# Optimizing a Trainium2 kernel written in Bass

```python
import numpy as np
import jax
import jax.numpy as jnp

def _softmax(x, axis=-1):
    return jax.nn.softmax(x, axis=axis)

def _gelu(x):
    return jax.nn.gelu(x, approximate=True)

def _silu(x):
    return jax.nn.silu(x)

def _sigmoid(x):
    return jax.nn.sigmoid(x)

def _layernorm(x, axis=-1, eps=1e-05):
    m = jnp.mean(x, axis=axis, keepdims=True)
    v = jnp.var(x, axis=axis, keepdims=True)
    return (x - m) / jnp.sqrt(v + eps)

def _scatter_add(tgt, idx, src, axis=0):
    return tgt.at[idx].add(src)

def _segment_sum(src, seg, n):
    return jax.ops.segment_sum(src, seg, n)
kernel_name = 'mk_lm_tower_d1_tok_ids768_r4_295233'

def setup_inputs(seed: int=0):
    np.random.seed(seed)
    _w = jnp.asarray

    def _rec_inputs():
        import jax
        import jax.numpy as jnp
        _rk = jax.random.key(seed)
        x = jax.random.randint(jax.random.fold_in(_rk, 1), (32, 256), 0, 31993, jnp.int32)
        mask_BS_i1_0 = jnp.where(jnp.ones((32, 256), dtype=bool), 1, 0).astype(jnp.int32)
        return (x, mask_BS_i1_0)
    x, mask_BS_i1_0 = _rec_inputs()

    def _L0_tok_setup():
        import jax, jax.numpy as jnp
        import numpy as np
        NH = 12
        W = 64
        EPS = 1e-12

        def layer_norm(x, s, b):
            mu = x.mean(-1, keepdims=True)
            var = ((x - mu) ** 2).mean(-1, keepdims=True)
            return (x - mu) / jnp.sqrt(var + EPS) * s + b

        def band_attention(q, k, v, mask):
            B, H, S, d = q.shape
            nc = S // W
            kp = jnp.pad(k, ((0, 0), (0, 0), (W, W), (0, 0)))
            vp = jnp.pad(v, ((0, 0), (0, 0), (W, W), (0, 0)))
            idx = jnp.arange(nc)[:, None] * W + jnp.arange(3 * W)[None, :]
            kb = kp[:, :, idx]
            vb = vp[:, :, idx]
            qc = q.reshape(B, H, nc, W, d)
            scores = jnp.einsum('bhcqd,bhckd->bhcqk', qc, kb) / jnp.sqrt(jnp.asarray(d, q.dtype))
            rel = jnp.arange(3 * W)[None, :] - W - jnp.arange(W)[:, None]
            band_ok = jnp.abs(rel) <= W
            key_abs = idx - W
            pos_ok = (key_abs >= 0) & (key_abs < S)
            mp = jnp.pad(mask, ((0, 0), (W, W)))
            mb = mp[:, idx] > 0
            allowed = mb[:, None, :, None, :] & pos_ok[None, None, :, None, :] & band_ok[None, None, None, :, :]
            scores = jnp.where(allowed, scores, jnp.asarray(-1000000000.0, scores.dtype))
            probs = jax.nn.softmax(scores, axis=-1)
            out = jnp.einsum('bhcqk,bhckd->bhcqd', probs, vb)
            return out.reshape(B, H, S, d)

        def _forward(input_ids, attention_mask, emb_word, emb_pos, emb_ln_s, emb_ln_b, Wq, bq, Wk, bk, Wv, bv, Wo, bo, ln1_s, ln1_b, W1, b1, W2, b2, ln2_s, ln2_b):
            B, S = input_ids.shape
            Hd = emb_word.shape[1]
            dh = Hd // NH
            mask = attention_mask.astype(emb_word.dtype)
            h = layer_norm(emb_word[input_ids] + emb_pos[:S][None], emb_ln_s, emb_ln_b)
            L = Wq.shape[0]
            for l in range(L):

                def heads(x):
                    return x.reshape(B, S, NH, dh).transpose(0, 2, 1, 3)
                q = heads(h @ Wq[l] + bq[l])
                k = heads(h @ Wk[l] + bk[l])
                v = heads(h @ Wv[l] + bv[l])
                a = band_attention(q, k, v, mask)
                a = a.transpose(0, 2, 1, 3).reshape(B, S, Hd)
                h = layer_norm(h + a @ Wo[l] + bo[l], ln1_s[l], ln1_b[l])
                f = jax.nn.gelu(h @ W1[l] + b1[l], approximate=False)
                h = layer_norm(h + f @ W2[l] + b2[l], ln2_s[l], ln2_b[l])
            return h
        key = jax.random.key(seed)
        B, S, Hd, L, V, FF = (2, 1024, 192, 4, 8000, 4 * 192)
        ks = jax.random.split(key, 16)
        std = 0.02
        inp = {'input_ids': jax.random.randint(ks[0], (B, S), 0, V, dtype=jnp.int64) if jax.config.jax_enable_x64 else jax.random.randint(ks[0], (B, S), 0, V, dtype=jnp.int32), 'attention_mask': jnp.ones((B, S), dtype=jnp.int32), 'emb_word': jax.random.normal(ks[1], (V, Hd), jnp.float32) * std, 'emb_pos': jax.random.normal(ks[2], (S, Hd), jnp.float32) * std, 'emb_ln_s': jnp.ones((Hd,), jnp.float32), 'emb_ln_b': jnp.zeros((Hd,), jnp.float32), 'Wq': jax.random.normal(ks[3], (L, Hd, Hd), jnp.float32) * std, 'bq': jnp.zeros((L, Hd), jnp.float32), 'Wk': jax.random.normal(ks[4], (L, Hd, Hd), jnp.float32) * std, 'bk': jnp.zeros((L, Hd), jnp.float32), 'Wv': jax.random.normal(ks[5], (L, Hd, Hd), jnp.float32) * std, 'bv': jnp.zeros((L, Hd), jnp.float32), 'Wo': jax.random.normal(ks[6], (L, Hd, Hd), jnp.float32) * std, 'bo': jnp.zeros((L, Hd), jnp.float32), 'ln1_s': jnp.ones((L, Hd), jnp.float32), 'ln1_b': jnp.zeros((L, Hd), jnp.float32), 'W1': jax.random.normal(ks[7], (L, Hd, FF), jnp.float32) * std, 'b1': jnp.zeros((L, FF), jnp.float32), 'W2': jax.random.normal(ks[8], (L, FF, Hd), jnp.float32) * std, 'b2': jnp.zeros((L, Hd), jnp.float32), 'ln2_s': jnp.ones((L, Hd), jnp.float32), 'ln2_b': jnp.zeros((L, Hd), jnp.float32)}
        return inp
    _L0_tok_all = _L0_tok_setup()
    _L0_tok_in = {k: v for k, v in _L0_tok_all.items() if k in ('emb_word', 'emb_pos', 'emb_ln_s', 'emb_ln_b', 'Wq', 'bq', 'Wk', 'bk', 'Wv', 'bv', 'Wo', 'bo', 'ln1_s', 'ln1_b', 'W1', 'b1', 'W2', 'b2', 'ln2_s', 'ln2_b')}
    del _L0_tok_all

    def _L0_attn_setup():
        import jax, jax.numpy as jnp
        import numpy as np
        N_HEAD = 12

        def _rotate_half(x):
            x_even = x[..., ::2]
            x_odd = x[..., 1::2]
            return jnp.stack((-x_odd, x_even), axis=-1).reshape(x.shape)

        def _rope_tables(T, D, dtype):
            inv_freq = 1.0 / 10000.0 ** (jnp.arange(0, D, 2, dtype=jnp.float32) / D)
            freqs = jnp.arange(T, dtype=jnp.float32)[:, None] * inv_freq[None, :]
            cos = jnp.repeat(jnp.cos(freqs), 2, axis=-1).astype(dtype)
            sin = jnp.repeat(jnp.sin(freqs), 2, axis=-1).astype(dtype)
            return (cos, sin)
        key = jax.random.key(seed)
        ks = jax.random.split(key, 5)
        B, T, C = (8, 256, 192)
        return {'x': jax.random.normal(ks[0], (B, T, C), dtype=jnp.float32), 'W_attn': jax.random.normal(ks[1], (C, 3 * C), dtype=jnp.float32) * C ** (-0.5), 'b_attn': jax.random.normal(ks[2], (3 * C,), dtype=jnp.float32) * 0.02, 'W_proj': jax.random.normal(ks[3], (C, C), dtype=jnp.float32) * C ** (-0.5), 'b_proj': jax.random.normal(ks[4], (C,), dtype=jnp.float32) * 0.02}
    _L0_attn_all = _L0_attn_setup()
    _L0_attn_in = {k: v for k, v in _L0_attn_all.items() if k in ('W_attn', 'b_attn', 'W_proj', 'b_proj')}
    del _L0_attn_all

    def _L0_ffn_setup():
        import math
        import jax, jax.numpy as jnp
        import numpy as np
        B, L, D = (8, 1024, 192)
        E = 16
        TOP_K = 2
        F_EXP = 4 * D
        F_SH = F_EXP * 2 // 4
        key = jax.random.key(seed)
        ks = jax.random.split(key, 8)
        s = lambda fan_in: 1.0 / math.sqrt(fan_in)
        return {'hidden_states': jax.random.normal(ks[0], (B, L, D), jnp.float32), 'gate_weight': jax.random.uniform(ks[1], (E, D), jnp.float32, -s(D), s(D)), 'Wg': jax.random.uniform(ks[2], (E, F_EXP, D), jnp.float32, -s(D), s(D)), 'Wu': jax.random.uniform(ks[3], (E, F_EXP, D), jnp.float32, -s(D), s(D)), 'Wd': jax.random.uniform(ks[4], (E, D, F_EXP), jnp.float32, -s(F_EXP), s(F_EXP)), 'Ws_g': jax.random.uniform(ks[5], (F_SH, D), jnp.float32, -s(D), s(D)), 'Ws_u': jax.random.uniform(ks[6], (F_SH, D), jnp.float32, -s(D), s(D)), 'Ws_d': jax.random.uniform(ks[7], (D, F_SH), jnp.float32, -s(F_SH), s(F_SH))}
    _L0_ffn_all = _L0_ffn_setup()
    _L0_ffn_in = {k: v for k, v in _L0_ffn_all.items() if k in ('gate_weight', 'Wg', 'Wu', 'Wd', 'Ws_g', 'Ws_u', 'Ws_d')}
    del _L0_ffn_all
    return {'x': x, 'mask_BS_i1_0': mask_BS_i1_0, 'L0_tok_emb_word': _L0_tok_in['emb_word'], 'L0_tok_emb_pos': _L0_tok_in['emb_pos'], 'L0_tok_emb_ln_s': _L0_tok_in['emb_ln_s'], 'L0_tok_emb_ln_b': _L0_tok_in['emb_ln_b'], 'L0_tok_Wq': _L0_tok_in['Wq'], 'L0_tok_bq': _L0_tok_in['bq'], 'L0_tok_Wk': _L0_tok_in['Wk'], 'L0_tok_bk': _L0_tok_in['bk'], 'L0_tok_Wv': _L0_tok_in['Wv'], 'L0_tok_bv': _L0_tok_in['bv'], 'L0_tok_Wo': _L0_tok_in['Wo'], 'L0_tok_bo': _L0_tok_in['bo'], 'L0_tok_ln1_s': _L0_tok_in['ln1_s'], 'L0_tok_ln1_b': _L0_tok_in['ln1_b'], 'L0_tok_W1': _L0_tok_in['W1'], 'L0_tok_b1': _L0_tok_in['b1'], 'L0_tok_W2': _L0_tok_in['W2'], 'L0_tok_b2': _L0_tok_in['b2'], 'L0_tok_ln2_s': _L0_tok_in['ln2_s'], 'L0_tok_ln2_b': _L0_tok_in['ln2_b'], 'L0_attn_W_attn': _L0_attn_in['W_attn'], 'L0_attn_b_attn': _L0_attn_in['b_attn'], 'L0_attn_W_proj': _L0_attn_in['W_proj'], 'L0_attn_b_proj': _L0_attn_in['b_proj'], 'L0_ffn_gate_weight': _L0_ffn_in['gate_weight'], 'L0_ffn_Wg': _L0_ffn_in['Wg'], 'L0_ffn_Wu': _L0_ffn_in['Wu'], 'L0_ffn_Wd': _L0_ffn_in['Wd'], 'L0_ffn_Ws_g': _L0_ffn_in['Ws_g'], 'L0_ffn_Ws_u': _L0_ffn_in['Ws_u'], 'L0_ffn_Ws_d': _L0_ffn_in['Ws_d']}

def reference(x, mask_BS_i1_0, L0_tok_emb_word, L0_tok_emb_pos, L0_tok_emb_ln_s, L0_tok_emb_ln_b, L0_tok_Wq, L0_tok_bq, L0_tok_Wk, L0_tok_bk, L0_tok_Wv, L0_tok_bv, L0_tok_Wo, L0_tok_bo, L0_tok_ln1_s, L0_tok_ln1_b, L0_tok_W1, L0_tok_b1, L0_tok_W2, L0_tok_b2, L0_tok_ln2_s, L0_tok_ln2_b, L0_attn_W_attn, L0_attn_b_attn, L0_attn_W_proj, L0_attn_b_proj, L0_ffn_gate_weight, L0_ffn_Wg, L0_ffn_Wu, L0_ffn_Wd, L0_ffn_Ws_g, L0_ffn_Ws_u, L0_ffn_Ws_d):
    import jax
    import jax.numpy as jnp

    def _L0_tok_ref(input_ids, attention_mask, emb_word, emb_pos, emb_ln_s, emb_ln_b, Wq, bq, Wk, bk, Wv, bv, Wo, bo, ln1_s, ln1_b, W1, b1, W2, b2, ln2_s, ln2_b):
        import jax, jax.numpy as jnp
        import numpy as np
        NH = 12
        W = 64
        EPS = 1e-12

        def layer_norm(x, s, b):
            mu = x.mean(-1, keepdims=True)
            var = ((x - mu) ** 2).mean(-1, keepdims=True)
            return (x - mu) / jnp.sqrt(var + EPS) * s + b

        def band_attention(q, k, v, mask):
            B, H, S, d = q.shape
            nc = S // W
            kp = jnp.pad(k, ((0, 0), (0, 0), (W, W), (0, 0)))
            vp = jnp.pad(v, ((0, 0), (0, 0), (W, W), (0, 0)))
            idx = jnp.arange(nc)[:, None] * W + jnp.arange(3 * W)[None, :]
            kb = kp[:, :, idx]
            vb = vp[:, :, idx]
            qc = q.reshape(B, H, nc, W, d)
            scores = jnp.einsum('bhcqd,bhckd->bhcqk', qc, kb) / jnp.sqrt(jnp.asarray(d, q.dtype))
            rel = jnp.arange(3 * W)[None, :] - W - jnp.arange(W)[:, None]
            band_ok = jnp.abs(rel) <= W
            key_abs = idx - W
            pos_ok = (key_abs >= 0) & (key_abs < S)
            mp = jnp.pad(mask, ((0, 0), (W, W)))
            mb = mp[:, idx] > 0
            allowed = mb[:, None, :, None, :] & pos_ok[None, None, :, None, :] & band_ok[None, None, None, :, :]
            scores = jnp.where(allowed, scores, jnp.asarray(-1000000000.0, scores.dtype))
            probs = jax.nn.softmax(scores, axis=-1)
            out = jnp.einsum('bhcqk,bhckd->bhcqd', probs, vb)
            return out.reshape(B, H, S, d)

        def _forward(input_ids, attention_mask, emb_word, emb_pos, emb_ln_s, emb_ln_b, Wq, bq, Wk, bk, Wv, bv, Wo, bo, ln1_s, ln1_b, W1, b1, W2, b2, ln2_s, ln2_b):
            B, S = input_ids.shape
            Hd = emb_word.shape[1]
            dh = Hd // NH
            mask = attention_mask.astype(emb_word.dtype)
            h = layer_norm(emb_word[input_ids] + emb_pos[:S][None], emb_ln_s, emb_ln_b)
            L = Wq.shape[0]
            for l in range(L):

                def heads(x):
                    return x.reshape(B, S, NH, dh).transpose(0, 2, 1, 3)
                q = heads(h @ Wq[l] + bq[l])
                k = heads(h @ Wk[l] + bk[l])
                v = heads(h @ Wv[l] + bv[l])
                a = band_attention(q, k, v, mask)
                a = a.transpose(0, 2, 1, 3).reshape(B, S, Hd)
                h = layer_norm(h + a @ Wo[l] + bo[l], ln1_s[l], ln1_b[l])
                f = jax.nn.gelu(h @ W1[l] + b1[l], approximate=False)
                h = layer_norm(h + f @ W2[l] + b2[l], ln2_s[l], ln2_b[l])
            return h
        return _forward(input_ids, attention_mask, emb_word, emb_pos, emb_ln_s, emb_ln_b, Wq, bq, Wk, bk, Wv, bv, Wo, bo, ln1_s, ln1_b, W1, b1, W2, b2, ln2_s, ln2_b)

    def _L0_attn_ref(x, W_attn, b_attn, W_proj, b_proj):
        import jax, jax.numpy as jnp
        import numpy as np
        N_HEAD = 12

        def _rotate_half(x):
            x_even = x[..., ::2]
            x_odd = x[..., 1::2]
            return jnp.stack((-x_odd, x_even), axis=-1).reshape(x.shape)

        def _rope_tables(T, D, dtype):
            inv_freq = 1.0 / 10000.0 ** (jnp.arange(0, D, 2, dtype=jnp.float32) / D)
            freqs = jnp.arange(T, dtype=jnp.float32)[:, None] * inv_freq[None, :]
            cos = jnp.repeat(jnp.cos(freqs), 2, axis=-1).astype(dtype)
            sin = jnp.repeat(jnp.sin(freqs), 2, axis=-1).astype(dtype)
            return (cos, sin)
        B, T, C = x.shape
        H = N_HEAD
        D = C // H
        qkv = x @ W_attn + b_attn
        q, k, v = jnp.split(qkv, 3, axis=-1)
        q = q.reshape(B, T, H, D).transpose(0, 2, 1, 3)
        k = k.reshape(B, T, H, D).transpose(0, 2, 1, 3)
        v = v.reshape(B, T, H, D).transpose(0, 2, 1, 3)
        cos, sin = _rope_tables(T, D, x.dtype)
        q = q * cos + _rotate_half(q) * sin
        k = k * cos + _rotate_half(k) * sin
        att = jnp.einsum('bhqd,bhkd->bhqk', q, k) * D ** (-0.5)
        causal = jnp.tril(jnp.ones((T, T), dtype=bool))
        att = jnp.where(causal, att, -jnp.inf)
        att = jax.nn.softmax(att, axis=-1)
        y = jnp.einsum('bhqk,bhkd->bhqd', att, v)
        y = y.transpose(0, 2, 1, 3).reshape(B, T, C)
        return y @ W_proj + b_proj

    def _L0_ffn_ref(hidden_states, gate_weight, Wg, Wu, Wd, Ws_g, Ws_u, Ws_d):
        import math
        import jax, jax.numpy as jnp
        import numpy as np
        B, L, D = (8, 1024, 192)
        E = 16
        TOP_K = 2
        F_EXP = 4 * D
        F_SH = F_EXP * 2 // 4
        b, l, d = hidden_states.shape
        n = b * l
        x = hidden_states.reshape(n, d)
        scores = jax.nn.sigmoid(x @ gate_weight.T)
        capacity = math.ceil(n / E * TOP_K)
        topk_score, topk_ids = jax.lax.top_k(scores.T, capacity)
        xg = x[topk_ids]
        gate = jax.nn.silu(jnp.einsum('ecd,efd->ecf', xg, Wg))
        up = jnp.einsum('ecd,efd->ecf', xg, Wu)
        out = jnp.einsum('ecf,edf->ecd', gate * up, Wd)
        out = out * topk_score[..., None]
        y = jnp.zeros((n, d), x.dtype).at[topk_ids.reshape(-1)].add(out.reshape(-1, d))
        y = y.reshape(b, l, d)
        shared = jax.nn.silu(hidden_states @ Ws_g.T) * (hidden_states @ Ws_u.T) @ Ws_d.T
        return y + shared
    h = _L0_tok_ref(x, mask_BS_i1_0, L0_tok_emb_word, L0_tok_emb_pos, L0_tok_emb_ln_s, L0_tok_emb_ln_b, L0_tok_Wq, L0_tok_bq, L0_tok_Wk, L0_tok_bk, L0_tok_Wv, L0_tok_bv, L0_tok_Wo, L0_tok_bo, L0_tok_ln1_s, L0_tok_ln1_b, L0_tok_W1, L0_tok_b1, L0_tok_W2, L0_tok_b2, L0_tok_ln2_s, L0_tok_ln2_b)
    h = h + _L0_attn_ref(_layernorm(h, axis=-1), L0_attn_W_attn, L0_attn_b_attn, L0_attn_W_proj, L0_attn_b_proj)
    h = h + _L0_ffn_ref(_layernorm(h, axis=-1), L0_ffn_gate_weight, L0_ffn_Wg, L0_ffn_Wu, L0_ffn_Wd, L0_ffn_Ws_g, L0_ffn_Ws_u, L0_ffn_Ws_d)
    return h

_drawn_inputs = setup_inputs


def setup_inputs(seed=0):
    import zlib

    import numpy as np

    out = dict(_drawn_inputs(seed))
    spreads = {'L0_tok_emb_ln_s': (1.0, 0.2),
     'L0_tok_emb_ln_b': (0.0, 0.1),
     'L0_tok_bq': (0.0, 0.8),
     'L0_tok_bk': (0.0, 0.8),
     'L0_tok_bv': (0.0, 0.1),
     'L0_tok_bo': (0.0, 0.1),
     'L0_tok_ln1_s': (1.0, 0.2),
     'L0_tok_ln1_b': (0.0, 0.1),
     'L0_tok_b1': (0.0, 0.1),
     'L0_tok_b2': (0.0, 0.1),
     'L0_tok_ln2_s': (1.0, 0.2),
     'L0_tok_ln2_b': (0.0, 0.1)}
    factors = {'L0_tok_Wq': 8.0, 'L0_tok_Wk': 8.0, 'L0_attn_b_attn': 3.201, 'L0_attn_b_proj': 3.584}
    for name, (base, spread) in spreads.items():
        noise = np.random.default_rng([zlib.crc32(name.encode()), seed]).standard_normal(out[name].shape)
        drawn = base * np.exp(spread * noise) if base else spread * noise
        out[name] = jnp.asarray(drawn.astype(out[name].dtype))
    for name, factor in factors.items():
        out[name] = (out[name] * factor).astype(out[name].dtype)
    return out
```

```python
import numpy as np
import concourse.bass as bass
from concourse import mybir
from contextlib import ExitStack

F32 = mybir.dt.float32
BF16 = mybir.dt.bfloat16
I32 = mybir.dt.int32
ALU = mybir.AluOpType
ACT = mybir.ActivationFunctionType
AX = mybir.AxisListType.X

P = 128
D = 192
DC = 96
NH = 12
DH = 16
S = 256
W = 64
T = S // P
FF = 768
FC = FF // P
FS = 384
FSC = FS // P
E = 16
NST = 2
SLOTS = 6
STK = P
XROW = D + E
NEG_BAND = -1.0e30
NEG_KEY = -1.0e30
M_FLOOR = -4.0e9
SCALE = 0.25
ST = (0, 1)

BAND_COLS = [(0, 0, 192), (192, 64, 192)]
CAUSAL_Q = [(0, 0, 128), (128, 0, 256)]
CAUSAL_K = [(0, 0, 256), (256, 128, 128)]
SCOLS = 384

TOK_LINKS = 18
CAUSAL_LINKS = 21


def constants():
    def cols(ranges, fn):
        m = np.zeros((P, SCOLS), np.float32)
        for t, (c, f0, w) in enumerate(ranges):
            part = (t * P + np.arange(P))[:, None]
            free = (f0 + np.arange(w))[None, :]
            m[:, c:c + w] = fn(part, free)
        return m

    band = lambda a, b: np.where(np.abs(a - b) <= W, 0.0, NEG_BAND)
    masks = np.stack([
        cols(BAND_COLS, band),
        cols(BAND_COLS, band),
        cols(CAUSAL_Q, lambda q, k: np.where(k <= q, 0.0, NEG_BAND)),
        cols(CAUSAL_K, lambda k, q: np.where(k <= q, 0.0, NEG_BAND)),
    ]).astype(np.float32)
    k = (np.arange(T)[None, :] * P + np.arange(P)[:, None])[:, :, None]
    q = np.arange(S)[None, None, :]
    window = (np.abs(k // W - q // W) <= 1).astype(np.float32) / (3 * W)
    inv = (1.0 / 10000.0 ** (np.arange(0, DH, 2, dtype=np.float32) / DH)).astype(np.float32)
    fr = np.arange(S, dtype=np.float32)[:, None] * inv[None, :]
    cos, sin = np.cos(fr).astype(np.float32), np.sin(fr).astype(np.float32)
    rope = np.zeros((P, T, 3, DH), np.float32)
    for t in range(T):
        rope[:, t, 0] = np.repeat(cos[t * P:(t + 1) * P], 2, axis=1)
        rope[:, t, 1, 0:8] = -sin[t * P:(t + 1) * P]
        rope[:, t, 2, 0:8] = sin[t * P:(t + 1) * P]
    return {"c_eye": np.eye(P, dtype=np.float32), "c_masks": masks, "c_window": window, "c_rope": rope}


def select_constants(n, seg):
    r = np.arange(P)
    same = (r[:, None] // seg == r[None, :] // seg)
    before = same & (r[:, None] < r[None, :])
    nblk = n // seg // P
    tile = (np.arange(seg)[None, :] * nblk + np.arange(nblk)[:, None]).astype(np.float32)
    bits = (1 << np.arange(29, -1, -1)).astype(np.int32)
    return {
        "c_same": same.astype(np.float32), "c_before": before.astype(np.float32),
        "c_bits": np.broadcast_to(bits[None], (P, 30)).copy(),
        "c_iota": np.broadcast_to(np.arange(32, dtype=np.float32)[None], (P, 32)).copy(),
        "c_part": np.arange(P, dtype=np.float32)[:, None].copy(),
        "c_tile": np.broadcast_to(tile.reshape(1, -1), (P, seg * nblk)).copy(),
    }


def wait_apart(eng, sem, value, held, held_value):
    eng.lower_val(value)
    eng.wait_ge(held, held_value)
    eng.wait_ge(sem, value)


class Semaphores:

    def __init__(self, nc):
        self.nc, self.all = nc, []

    def __call__(self, name):
        self.all.append(self.nc.alloc_semaphore(name))
        return self.all[-1]

    def lift(self, sems):
        for s in sems:
            self.nc.sync.sem_inc(s, 1)
        self.nc.all_engine_barrier()

    def close(self):
        self.nc.clear_and_free_semaphores(self.all)
        self.nc.all_engine_barrier()
        self.all = []


class Phase:

    def __init__(self, sems, counts, tag, lifted):
        self.n, self.lifted = counts, lifted
        self.sem = {k: [sems(f"{tag}_{k}{s}") for s in ST] for k in counts}
        sems.lift([x for k in lifted for x in self.sem[k]])

    def value(self, key, it, k=None):
        n = self.n[key]
        return it * n + ((n if k is None else k) + (key in self.lifted))

    def wait(self, eng, key, s, it, k=None):
        assert k != 0 or key in self.lifted, key
        eng.wait_ge(self.sem[key][s], self.value(key, it, k))

    def wait_apart(self, eng, key, s, it, k, held, held_value):
        wait_apart(eng, self.sem[key][s], self.value(key, it, k), held, held_value)

    def inc(self, ins, key, s):
        ins.then_inc(self.sem[key][s], 16 if key in ("h_in", "am_in", "h_st", "x_st", "y_st", "s_st") else 1)


def build(nc, a, out, B, L, V):
    ctx = ExitStack()
    with ctx:
        N = B * S
        NT = N // P
        PAIRS = B // NST
        NIT = L * PAIRS
        CAP = N // E * 2
        hbuf = nc.dram_tensor("hbuf", [(L + 1) * N + NST * S, D], F32, kind="Internal").ap()
        xs = nc.dram_tensor("xs", [N, XROW], F32, kind="Internal").ap()
        sd = nc.dram_tensor("sd", [E, N], F32, kind="Internal").ap()
        am_d = nc.dram_tensor("am_d", [B + NST, S], F32, kind="Internal").ap()
        ids_d = nc.dram_tensor("ids_d", [E, CAP], I32, kind="Internal").ap()
        embed(nc, a, hbuf, am_d, B, V, (L + 1) * N)
        tower(nc, a, hbuf, am_d, xs, sd, out, B, L)
        choose(nc, a, sd, ids_d, N, CAP)
        experts(nc, a, xs, ids_d, out, N, CAP)


def embed(nc, a, hbuf, am_d, B, V, HROWS):
    N = B * S
    NT = N // P
    G = 4
    STEPS = NT // G
    MASK_LINKS = 11
    with ExitStack() as ctx:
        sb = lambda name, shape, dt: ctx.enter_context(nc.sbuf_tensor("emb_" + name, shape, dt))
        sem = Semaphores(nc)
        ids_raw = sb("ids_raw", [P, NT], I32)
        idf = sb("idf", [P, NT], F32)
        neg = sb("neg", [P, NT], F32)
        ids = sb("ids", [P, NT], I32)
        emb = sb("emb", [P, NT, D], F32)
        pos = sb("pos", [P, T, D], F32)
        lnw = sb("lnw", [P, 2 * D], F32)
        st = sb("st", [P, G, 6], F32)
        mv = sb("mv", [P, G, 2], F32)
        ve = sb("ve", [P, G], F32)
        half = sb("half", [P, G], F32)
        rstd = sb("rstd", [P, G], F32)
        z = sb("z", [P, G, D], F32)
        mi = sb("mi", [B, S], I32)
        PADW = S + 2 * W
        mw = [sb("mw0", [B, PADW], F32), sb("mw1", [B, PADW], F32)]
        in_sem, row_sem, mask_sem, am_st = sem("e_in"), sem("e_row"), sem("e_mask"), sem("e_amst")
        ids_ok, gathered = sem("e_ids"), [sem(f"e_gath{g}") for g in range(STEPS)]
        chain, var_ok, rstd_ok, z_ok, z_out, const_ok = (sem("e_chain"), sem("e_var"), sem("e_rstd"),
                                                         sem("e_z"), sem("e_zout"), sem("e_const"))
        ctx.callback(sem.close)
        block = ctx.enter_context(nc.Block())

        @block.sync
        def _(sp):
            sp.dma_start(ids_raw[:], a["x"].rearrange("b (t p) -> p (b t)", p=P), allow_slow_non_contiguous=True).then_inc(in_sem, 16)
            sp.dma_start(pos[:], a["emb_pos"].rearrange("(t p) d -> p t d", p=P)).then_inc(row_sem, 16)
            sp.dma_start(lnw[:], a["emb_ln"].to_broadcast([P, 2 * D])).then_inc(row_sem, 16)
            sp.dma_start(mi[:], a["mask"]).then_inc(mask_sem, 16)
            sp.wait_ge(chain, MASK_LINKS)
            sp.dma_start(am_d[0:B, :], mw[0][:, 0:S]).then_inc(am_st, 16)
            sp.dma_start(am_d[B:B + NST, :], mw[0][0:NST, 0:S]).then_inc(am_st, 16)
            for g in range(STEPS):
                sp.wait_ge(z_ok, g + 1)
                rows = hbuf[g * G * P:(g + 1) * G * P, :]
                sp.dma_start(rows.rearrange("(t p) d -> p t d", p=P), z[:]).then_inc(z_out, 16)
                if g == 0:
                    rows = hbuf[HROWS:HROWS + G * P, :]
                    sp.dma_start(rows.rearrange("(t p) d -> p t d", p=P), z[:]).then_inc(z_out, 16)
            sp.wait_ge(z_out, 16 * (STEPS + 1))
            sp.wait_ge(am_st, 32)

        @block.gpsimd
        def _(pool):
            nc.gpsimd.memset(half[:], -0.5).then_inc(const_ok, 1)
            pool.wait_ge(ids_ok, 1)
            for t in range(NT):
                pool.indirect_dma_start(emb[:, t, :], None, a["emb_word"],
                                        bass.IndirectOffsetOnAxis(ap=ids[:, t:t + 1], axis=0)
                                        ).then_inc(gathered[t // G], 16)
            pool.wait_ge(const_ok, 1)
            for g in range(STEPS):
                pool.wait_ge(var_ok, g + 1)
                nc.gpsimd.tensor_tensor(rstd[:], ve[:], half[:], ALU.pow).then_inc(rstd_ok, 1)

        @block.vector
        def _(dve):
            n = [0]

            def link(ins):
                n[0] += 1
                ins.then_inc(chain, 1)
                dve.wait_ge(chain, n[0])

            link(nc.vector.memset(mw[0][:], 0.0))
            dve.wait_ge(mask_sem, 16)
            link(nc.vector.tensor_scalar(mw[0][:, W:W + S], mi[:], 0, None, ALU.is_gt))
            src = 0
            for sh in (1, 2, 4, 8, 16, 32, 64):
                width = PADW - sh
                nc.vector.tensor_copy(mw[1 - src][:, width:PADW], mw[src][:, width:PADW])
                link(nc.vector.tensor_tensor(mw[1 - src][:, 0:width], mw[src][:, 0:width],
                                             mw[src][:, sh:sh + width], ALU.max))
                src = 1 - src
            link(nc.vector.tensor_tensor(mw[0][:, 0:S], mw[1][:, 0:S], mw[1][:, 1:S + 1], ALU.max))
            link(nc.vector.tensor_scalar(mw[0][:, 0:S], mw[0][:, 0:S], -1.0, 1.0, ALU.mult, ALU.add))
            assert n[0] == MASK_LINKS, n
            dve.wait_ge(in_sem, 16)
            link(nc.vector.tensor_copy(idf[:], ids_raw[:]))
            link(nc.vector.tensor_scalar(neg[:], idf[:], 0.0, float(V), ALU.is_lt, ALU.mult))
            link(nc.vector.tensor_tensor(idf[:], idf[:], neg[:], ALU.add))
            link(nc.vector.tensor_scalar(idf[:], idf[:], 0.0, float(V - 1), ALU.max, ALU.min))
            nc.vector.tensor_copy(ids[:], idf[:]).then_inc(ids_ok, 1)
            dve.wait_ge(row_sem, 32)
            for g in range(STEPS):
                e = emb[:, g * G:(g + 1) * G, :]
                e4 = emb[:, g * G:(g + 1) * G, :].rearrange("p (c t) d -> p c t d", t=T)
                dve.wait_ge(gathered[g], 16 * G)
                link(nc.vector.tensor_tensor(e4, e4, pos[:].unsqueeze(1).to_broadcast([P, G // T, T, D]), ALU.add))
                for t in range(G):
                    last = nc.vector.bn_stats(st[:, t, :], e[:, t, :])
                link(last)
                for t in range(G):
                    last = nc.vector.bn_aggr(mv[:, t, :], st[:, t, :])
                link(last)
                if g > 0:
                    dve.wait_ge(rstd_ok, g)
                nc.vector.tensor_scalar(ve[:], mv[:, :, 1], 1e-12, None, ALU.add).then_inc(var_ok, 1)
                dve.wait_ge(rstd_ok, g + 1)
                if g > 0:
                    dve.wait_ge(z_out, 16 * (g + 1))
                for t in range(G):
                    last = nc.vector.tensor_scalar(z[:, t, :], e[:, t, :], mv[:, t, 0:1], rstd[:, t:t + 1],
                                                   ALU.subtract, ALU.mult)
                link(last)
                link(nc.vector.tensor_tensor(z[:], z[:], lnw[:, 0:D].unsqueeze(1).to_broadcast([P, G, D]), ALU.mult))
                nc.vector.tensor_tensor(z[:], z[:], lnw[:, D:2 * D].unsqueeze(1).to_broadcast([P, G, D]),
                                        ALU.add).then_inc(z_ok, 1)


def tower(nc, a, hbuf, am_d, xs, sd, out, B, L):
    N = B * S
    NT = N // P
    PAIRS = B // NST
    NIT = L * PAIRS
    VEC = 3 * D + 6 * D
    with ExitStack() as ctx:
        sb = lambda name, shape, dt: ctx.enter_context(nc.sbuf_tensor(name, shape, dt))
        sbs = lambda name, shape, dt: [sb(f"{name}{s}", shape, dt) for s in ST]
        sem = Semaphores(nc)

        bank = [[ctx.enter_context(nc.psum_tensor(f"bank{s}{i}", [P, 512], F32)) for i in range(4)] for s in ST]

        wqkv = sb("wqkv", [DC, 2, 3 * D], F32)
        wo = sb("wo", [DC, 2, D], F32)
        w1 = sb("w1", [DC, 2, FF], F32)
        w2 = sb("w2", [P, FC, D], F32)
        vec = sb("vec", [P, VEC], F32)
        b1 = sb("b1", [P, FC], F32)
        BO, L1S, L1B, B2, L2S, L2B = (3 * D + i * D for i in range(6))
        wide = lambda at: vec[:, at:at + D].unsqueeze(1).to_broadcast([P, T, D])

        eye = sb("eye", [P, P], F32)
        eyeb = sb("eyeb", [P, P], BF16)
        maskf = sb("maskf", [P, 4, SCOLS], F32)
        maskb = sb("maskb", [P, 4, SCOLS], BF16)
        window = sb("window", [P, T, S], F32)
        rope = sb("rope", [P, T, 3, DH], F32)
        kb_i = sb("kb_i", [P, NT], I32)
        kb = sb("kb", [P, NT + 2 * NST * T], F32)
        amc = sb("amc", [P, NT], F32)
        half = sb("half", [P, T], F32)

        hcur = sbs("hcur", [P, T, D], F32)
        hT = sbs("hT", [DC, 2, S], F32)
        qk = sbs("qk", [P, T, 2, NH, DH], F32)
        rem = sbs("rem", [P, T, 2, NH, DH], F32)
        vaug = sbs("vaug", [P, T, NH, 32], F32)
        stack = sbs("stack", [P, T, 2, NH, STK], BF16)
        qT = sbs("qT", [P, NH, S], BF16)
        kT = sbs("kT", [P, NH, S], BF16)
        mx = sbs("mx", [P, T, NH], F32)
        mrow = sbs("mrow", [P, T, NH, 32], BF16)
        NPT = 4
        pT = sbs("pT", [P, NPT, SCOLS], F32)
        amb = sbs("amb", [P, S], F32)
        wam = sbs("wam", [P, T, S], F32)
        den = sbs("den", [P, T, NH], F32)
        att = sbs("att", [P, T, D], F32)
        resid = sbs("resid", [P, T, D], F32)
        h1 = sbs("h1", [P, T, D], F32)
        hout = sbs("hout", [P, T, D], F32)
        stt = sbs("stt", [P, T, 6], F32)
        mv = sbs("mv", [P, T, 2], F32)
        ve = sbs("ve", [P, T], F32)
        rstd = sbs("rstd", [P, T], F32)
        gw = sb("gw", [DC, 2, E], F32)
        xr = sbs("xr", [P, T, XROW], F32)
        sig = sbs("sig", [P, T, E], F32)
        sT = sbs("sT", [E, S], F32)

        w_in = sem("w_in")
        c_in, c_ok, kb_ok, half_ok = sem("c_in"), sem("c_ok"), sem("kb_ok"), sem("half_ok")

        common = dict(
            h_in=16, hT_ps=1, hT=1, qk_ps=2, v_ps=1, qk=2, v=1, stk=1, fill=6, ev_v=3, ev_s=3,
            sc1=NH, mx=NH, m=1, mT_ps=3, mT=3, sc2=NH, p=NH, pv=NH, ot=1, otT_ps=2, att=1,
            aT_ps=1, aT=1, wo_ps=1, var1=1, rstd1=1, h1=1, h1T_ps=1, h1T=1)
        ctx.callback(sem.close)
        layer_sems = Semaphores(nc)
        tok = Phase(layer_sems, dict(
            common, am_in=16, wam=1, u_ps=1, hb=2, w1_ps=3, g=FC, w2_ps=1, var2=1, rstd2=1, h2=1,
            h_st=16, dve=TOK_LINKS), "t", ("h2", "h_st"))

        def pe_transposes(src, dst, key, s, ready=None):
            for c in range(2):
                for t in range(T):
                    last = nc.tensor.transpose(dst[0:DC, c * S + t * P:c * S + (t + 1) * P],
                                               src[:, t, c * DC:(c + 1) * DC], eye[:])
            return last

        def attention_pe(ph, pe, it, src, src_key, ff_src, bank3_key, masks, qcols, kcols, banded):
            for s in ST:
                ph.wait(pe, src_key, s, it)
                ph.inc(pe_transposes(src[s], bank[s][0], None, s), "hT_ps", s)
            for s in ST:
                b = bank[s]
                ph.wait(pe, "hT", s, it)
                ph.wait(pe, bank3_key, s, it, 0)
                for t in range(T):
                    for c in range(2):
                        last = nc.tensor.matmul(b[1 + t][:, 0:2 * D], hT[s][:, c, t * P:(t + 1) * P],
                                                wqkv[:, c, 0:2 * D], start=(c == 0), stop=(c == 1))
                    ph.inc(last, "qk_ps", s)
                for t in range(T):
                    for c in range(2):
                        last = nc.tensor.matmul(b[3][:, t * D:(t + 1) * D], hT[s][:, c, t * P:(t + 1) * P],
                                                wqkv[:, c, 2 * D:3 * D], start=(c == 0), stop=(c == 1))
                ph.inc(last, "v_ps", s)
            for f in range(6):
                for s in ST:
                    if f == 0:
                        ph.wait(pe, "stk", s, it)
                        ph.wait(pe, "v", s, it)
                    if f == 4:
                        ph.wait(pe, "ev_v", s, it, 1)
                    if f == 5:
                        ph.wait(pe, "ev_s", s, it, 1)
                    dst = bank[s][f % 4][:].bitcast(BF16)
                    side, h0 = f // 3, (f % 3) * 4
                    for j in range(4):
                        for t in range(T):
                            last = nc.tensor.transpose(dst[:, j * S + t * P:j * S + (t + 1) * P],
                                                       stack[s][:, t, side, h0 + j, :], eyeb[:])
                    ph.inc(last, "fill", s)
            for h in range(NH):
                for s in ST:
                    if h == 0:
                        ph.wait(pe, "ev_v", s, it)
                        ph.wait(pe, "ev_s", s, it)
                    if h >= 2:
                        ph.wait(pe, "mx", s, it, h - 1)
                    dst = bank[s][h % 2]
                    nc.tensor.matmul(dst[:, 0:SCOLS], eyeb[:], maskb[:, masks, :], start=True, stop=False)
                    for t, (c0, f0, w) in enumerate(qcols):
                        last = nc.tensor.matmul(dst[:, c0:c0 + w], qT[s][:, h, t * P:(t + 1) * P],
                                                kT[s][:, h, f0:f0 + w], start=False, stop=(t == T - 1))
                    ph.inc(last, "sc1", s)
            for f in range(3):
                for s in ST:
                    if f == 0:
                        ph.wait(pe, "m", s, it)
                    dst = bank[s][f][:].bitcast(BF16)
                    for j in range(4):
                        for t in range(T):
                            last = nc.tensor.transpose(dst[DC:P, j * S + t * P:j * S + (t + 1) * P],
                                                       mrow[s][:, t, f * 4 + j, :], eyeb[:],
                                                       tile_position=(0, DC))
                    ph.inc(last, "mT_ps", s)

            def product(h, s):
                ph.wait(pe, "p", s, it, h + 1)
                g, j = h // 4, h % 4
                dst = bank[s][2 + g // 2]
                at = (g % 2) * S
                (_, _, w0), (c1, f1, w1_) = kcols
                parts = [(0, 0, 0, w0), (1, c1, f1, w0 - f1), (1, c1 + w0 - f1, w0, f1 + w1_ - w0)]
                parts = [part for part in parts if part[3]]
                for n, (t, c0, f0, w) in enumerate(parts):
                    last = nc.tensor.matmul(dst[32 * j:32 * j + 32, at + f0:at + f0 + w],
                                            vaug[s][:, t, h, :], pT[s][:, h % NPT, c0:c0 + w],
                                            start=(n == 0), stop=(n == len(parts) - 1), tile_position=(0, 32 * j))
                ph.inc(last, "pv", s)

            for h in range(NH + 1):
                for s in ST:
                    if h < NH:
                        if h == 0:
                            ph.wait(pe, "mT", s, it)
                        if h >= 2:
                            ph.wait(pe, "p", s, it, h - 1)
                        dst = bank[s][h % 2]
                        nc.tensor.matmul(dst[:, 0:SCOLS], eyeb[:], maskb[:, masks + 1, :], start=True, stop=False)
                        for t, (c0, f0, w) in enumerate(kcols):
                            last = nc.tensor.matmul(dst[:, c0:c0 + w], kT[s][:, h, t * P:(t + 1) * P],
                                                    qT[s][:, h, f0:f0 + w], start=False, stop=(t == T - 1))
                        ph.inc(last, "sc2", s)
                    if h >= 1:
                        product(h - 1, s)
            if banded:
                for s in ST:
                    ph.wait(pe, "wam", s, it)
                    for t in range(T):
                        for k in range(T):
                            last = nc.tensor.matmul(
                                bank[s][0][:, t * D:(t + 1) * D], wam[s][:, k, t * P:(t + 1) * P],
                                vaug[s][:, k, :, 0:DH], start=(k == 0), stop=(k == T - 1))
                    ph.inc(last, "u_ps", s)
            for s in ST:
                oT = qk[s][:].rearrange("p t s h d -> p (t s h d)")
                ph.wait(pe, "ot", s, it)
                for t in range(T):
                    for g in range(3):
                        last = nc.tensor.transpose(bank[s][1 + t][:, g * P:(g + 1) * P],
                                                   oT[:, g * S + t * P:g * S + (t + 1) * P], eye[:])
                    ph.inc(last, "otT_ps", s)
            for s in ST:
                ph.wait(pe, "att", s, it)
                ph.inc(pe_transposes(att[s], bank[s][3], None, s), "aT_ps", s)
            for s in ST:
                ph.wait(pe, "aT", s, it)
                for t in range(T):
                    for c in range(2):
                        last = nc.tensor.matmul(bank[s][1][:, t * D:(t + 1) * D], hT[s][:, c, t * P:(t + 1) * P],
                                                wo[:, c, :], start=(c == 0), stop=(c == 1))
                ph.inc(last, "wo_ps", s)
            for s in ST:
                ph.wait(pe, "h1", s, it)
                ph.inc(pe_transposes(ff_src[s], bank[s][3], None, s), "h1T_ps", s)

        def attention_act(ph, act, it):
            for s in ST:
                ph.wait(act, "hT_ps", s, it)
                ph.inc(nc.scalar.copy(hT[s][:], bank[s][0][0:DC, :]), "hT", s)
            for f in (1, 3, 5):
                for s in ST:
                    dst = (qT if f < 3 else kT)[s][:, (f % 3) * 4:(f % 3) * 4 + 4, :]
                    ph.wait(act, "fill", s, it, f + 1)
                    ph.inc(nc.scalar.copy(dst, bank[s][f % 4][:].bitcast(BF16)), "ev_s", s)
            for f in range(3):
                for s in ST:
                    ph.wait(act, "mT_ps", s, it, f + 1)
                    ph.inc(nc.scalar.copy(qT[s][DC:P, f * 4:f * 4 + 4, :], bank[s][f][DC:P, :].bitcast(BF16)),
                           "mT", s)
            for h in range(NH):
                for s in ST:
                    ph.wait(act, "sc2", s, it, h + 1)
                    if h >= NPT:
                        ph.wait(act, "pv", s, it, h - NPT + 1)
                    ph.inc(nc.scalar.activation(pT[s][:, h % NPT, :], bank[s][h % 2][:, 0:SCOLS], ACT.Exp,
                                                scale=SCALE), "p", s)
            for s in ST:
                oT = qk[s][:].rearrange("p t s h d -> p (t s h d)")
                ph.wait(act, "pv", s, it)
                nc.scalar.copy(oT[:, 0:2 * S], bank[s][2][:])
                ph.inc(nc.scalar.copy(oT[:, 2 * S:3 * S], bank[s][3][:, 0:S]), "ot", s)
            for s in ST:
                ph.wait(act, "aT_ps", s, it)
                ph.inc(nc.scalar.copy(hT[s][:], bank[s][3][0:DC, :]), "aT", s)
            for s in ST:
                ph.wait(act, "h1T_ps", s, it)
                ph.inc(nc.scalar.copy(hT[s][:], bank[s][3][0:DC, :]), "h1T", s)

        class Chain:

            def __init__(self, ph, dve, it):
                self.ph, self.dve, self.it, self.k = ph, dve, it, [0, 0]

            def inc(self, ins, s):
                self.k[s] += 1
                ins.then_inc(self.ph.sem["dve"][s], 1)

            def value(self, s):
                return self.it * self.ph.n["dve"] + self.k[s]

            def wait(self, s):
                self.dve.wait_ge(self.ph.sem["dve"][s], self.value(s))

            def each(self, fn, before=None):
                for s in ST:
                    if before:
                        wait_apart(self.dve, self.ph.sem["dve"][s], self.value(s), before, 9)
                    elif self.k[s]:
                        self.wait(s)
                    self.inc(fn(s), s)

            def end(self):
                assert self.k[0] == self.k[1] == self.ph.n["dve"], self.k

        def norm_dve(ph, ch, it, x, dst, key, affine):
            def stats(s):
                nc.vector.bn_stats(stt[s][:, 0, :], x[s][:, 0, :])
                return nc.vector.bn_stats(stt[s][:, 1, :], x[s][:, 1, :])

            def aggr(s):
                nc.vector.bn_aggr(mv[s][:, 0, :], stt[s][:, 0, :])
                return nc.vector.bn_aggr(mv[s][:, 1, :], stt[s][:, 1, :])
            ch.each(stats)
            ch.each(aggr, c_ok)
            for s in ST:
                ch.wait(s)
                ph.inc(nc.vector.tensor_scalar(ve[s][:], mv[s][:, :, 1], affine[2], None, ALU.add), "var" + key, s)
            for s in ST:
                ph.wait(ch.dve, "rstd" + key, s, it)
                for t in range(T):
                    last = nc.vector.tensor_scalar(dst[s][:, t, :], x[s][:, t, :], mv[s][:, t, 0:1],
                                                   rstd[s][:, t:t + 1], ALU.subtract, ALU.mult)
                ch.inc(last, s) if affine[0] is not None else ph.inc(last, affine[3], s)
            if affine[0] is not None:
                ch.each(lambda s: nc.vector.tensor_tensor(dst[s][:], dst[s][:], wide(affine[0]), ALU.mult))
                for s in ST:
                    ch.wait(s)
                    ph.inc(nc.vector.tensor_tensor(dst[s][:], dst[s][:], wide(affine[1]), ALU.add), affine[3], s)

        def attention_dve(ph, ch, dve, it, kbcol, qcols, banded, rotary):
            flat = lambda x: x[:].rearrange("p t s h d -> p (t s h) d")
            for t in range(T):
                for s in ST:
                    ph.wait(dve, "qk_ps", s, it, t + 1)
                    ph.inc(nc.vector.tensor_tensor(qk[s][:, t].rearrange("p s h d -> p (s h d)"),
                                                   bank[s][1 + t][:, 0:2 * D], vec[:, 0:2 * D], ALU.add), "qk", s)
            for s in ST:
                ph.wait(dve, "v_ps", s, it)
                ph.inc(nc.vector.tensor_tensor(
                    vaug[s][:, :, :, 0:DH],
                    bank[s][3][:, 0:2 * D].rearrange("p (t h d) -> p t h d", t=T, h=NH),
                    vec[:, 2 * D:3 * D].rearrange("p (h d) -> p h d", h=NH).unsqueeze(1).to_broadcast([P, T, NH, DH]),
                    ALU.add), "v", s)
            for s in ST:
                ph.wait(dve, "qk", s, it)
            if rotary:
                def halves(x, s, o):
                    return x[s][:].rearrange("p t s h (i e) -> p t (s h) i e", e=2)[:, :, :, :, o]

                def sin(s, o):
                    return rope[:, :, 1 + o, 0:8].unsqueeze(2).to_broadcast([P, T, 2 * NH, 8])
                tmp = [pT[s][:].rearrange("p a b -> p (a b)")[:, 0:T * 2 * D]
                       .rearrange("p (t s h d) -> p t s h d", t=T, s=2, h=NH) for s in ST]
                for t in range(T):
                    ch.each(lambda s: nc.vector.tensor_tensor(
                        tmp[s][:, t].rearrange("p s h (i e) -> p (s h) i e", e=2)[:, :, :, 0],
                        qk[s][:, t].rearrange("p s h (i e) -> p (s h) i e", e=2)[:, :, :, 1],
                        rope[:, t, 1, 0:8].unsqueeze(1).to_broadcast([P, 2 * NH, 8]), ALU.mult))
                    ch.each(lambda s: nc.vector.tensor_tensor(
                        tmp[s][:, t].rearrange("p s h (i e) -> p (s h) i e", e=2)[:, :, :, 1],
                        qk[s][:, t].rearrange("p s h (i e) -> p (s h) i e", e=2)[:, :, :, 0],
                        rope[:, t, 2, 0:8].unsqueeze(1).to_broadcast([P, 2 * NH, 8]), ALU.mult))
                    ch.each(lambda s: nc.vector.tensor_tensor(
                        qk[s][:, t].rearrange("p s h d -> p (s h) d"), qk[s][:, t].rearrange("p s h d -> p (s h) d"),
                        rope[:, t, 0, :].unsqueeze(1).to_broadcast([P, 2 * NH, DH]), ALU.mult))
                    ch.each(lambda s: nc.vector.tensor_tensor(
                        qk[s][:, t].rearrange("p s h d -> p (s h d)"), qk[s][:, t].rearrange("p s h d -> p (s h d)"),
                        tmp[s][:, t].rearrange("p s h d -> p (s h d)"), ALU.add))
            sl = lambda s, i: stack[s][:].rearrange("p t s h (m d) -> p (t s h) m d", d=DH)[:, :, i, :]
            side = lambda s, w: stack[s][:, :, w].rearrange("p t h (m d) -> p t h m d", d=DH)
            ch.each(lambda s: nc.vector.tensor_copy(sl(s, 0), flat(qk[s])))
            ch.each(lambda s: nc.vector.tensor_tensor(flat(rem[s]), flat(qk[s]), sl(s, 0), ALU.subtract))
            ch.each(lambda s: nc.vector.tensor_copy(sl(s, 1), flat(rem[s])))

            def third(s):
                nc.vector.tensor_tensor(side(s, 0)[:, :, :, 5], rem[s][:, :, 0], side(s, 0)[:, :, :, 1], ALU.subtract)
                nc.vector.tensor_tensor(side(s, 1)[:, :, :, 4], rem[s][:, :, 1], side(s, 1)[:, :, :, 1], ALU.subtract)
                for w, dst, src in ((0, 2, 0), (0, 4, 0), (0, 3, 1), (1, 3, 0), (1, 5, 0), (1, 2, 1)):
                    nc.vector.tensor_copy(side(s, w)[:, :, :, dst], side(s, w)[:, :, :, src])
                return nc.vector.tensor_copy(
                    stack[s][:, :, 1, :, DC], kbcol(s).unsqueeze(2).to_broadcast([P, T, NH]))
            for s in ST:
                ch.wait(s)
                ph.inc(third(s), "stk", s)
            if banded:
                for s in ST:
                    ph.wait(dve, "am_in", s, it)
                    ph.inc(nc.vector.tensor_tensor(wam[s][:], window[:],
                                                   amb[s][:].unsqueeze(1).to_broadcast([P, T, S]), ALU.mult), "wam", s)
            for f in (0, 2, 4):
                for s in ST:
                    dst = (qT if f < 3 else kT)[s][:, (f % 3) * 4:(f % 3) * 4 + 4, :]
                    ph.wait(dve, "fill", s, it, f + 1)
                    ph.inc(nc.vector.tensor_copy(dst, bank[s][f % 4][:].bitcast(BF16)), "ev_v", s)
            for h in range(NH):
                for s in ST:
                    ph.wait(dve, "sc1", s, it, h + 1)
                    src = bank[s][h % 2]
                    if banded:
                        last = nc.vector.tensor_reduce(mx[s][:, :, h], src[:, 0:SCOLS].rearrange("p (t k) -> p t k", t=T),
                                                       AX, ALU.max)
                    else:
                        for t, (c0, _, w) in enumerate(qcols):
                            last = nc.vector.tensor_reduce(mx[s][:, t, h:h + 1], src[:, c0:c0 + w], AX, ALU.max)
                    ph.inc(last, "mx", s)
            for s in ST:
                ph.wait(dve, "mx", s, it)
                ch.inc(nc.vector.tensor_scalar(mx[s][:], mx[s][:], M_FLOOR, None, ALU.max), s)
            ch.each(lambda s: nc.vector.tensor_copy(mrow[s][:, :, :, 1], mx[s][:]))
            for s in ST:
                ch.wait(s)
                ph.inc(nc.vector.tensor_tensor(mrow[s][:, :, :, 2], mx[s][:], mrow[s][:, :, :, 1], ALU.subtract), "m", s)
            oTt = lambda s, t: bank[s][1 + t][:, 0:SCOLS].rearrange("p (h d) -> p h d", d=32)
            for s in ST:
                ph.wait(dve, "otT_ps", s, it)
                for t in range(T):
                    if banded:
                        last = nc.vector.tensor_scalar(den[s][:, t], oTt(s, t)[:, :, DH], kbcol(s, True)[:, t:t + 1],
                                                       None, ALU.add)
                    else:
                        last = nc.vector.tensor_copy(den[s][:, t], oTt(s, t)[:, :, DH])
                ch.inc(last, s)
            ch.each(lambda s: nc.vector.reciprocal(den[s][:], den[s][:]))
            for s in ST:
                ch.wait(s)
                for t in range(T):
                    last = nc.vector.tensor_tensor(att[s][:, t].rearrange("p (h d) -> p h d", d=DH),
                                                   oTt(s, t)[:, :, 0:DH],
                                                   den[s][:, t].unsqueeze(2).to_broadcast([P, NH, DH]), ALU.mult)
                if banded:
                    ch.inc(last, s)
                else:
                    ph.inc(last, "att", s)
            if banded:
                for s in ST:
                    ch.wait(s)
                    ph.wait(dve, "u_ps", s, it)
                    ph.inc(nc.vector.tensor_tensor(att[s][:].rearrange("p t d -> p (t d)"),
                                                   att[s][:].rearrange("p t d -> p (t d)"),
                                                   bank[s][0][:, 0:2 * D], ALU.add), "att", s)

        def setup_dve(dve):
            dve.wait_ge(c_in, 16 * 6)
            nc.vector.tensor_copy(eyeb[:], eye[:]).then_inc(c_ok, 1)
            nc.vector.tensor_copy(maskb[:], maskf[:]).then_inc(c_ok, 1)
            nc.vector.memset(kb[:, NT:], 0.0).then_inc(c_ok, 1)
            nc.vector.tensor_scalar(kb[:, 0:NT], kb_i[:], 0, -NEG_KEY, ALU.is_gt, ALU.mult).then_inc(kb_ok, 1)
            dve.wait_ge(kb_ok, 1)
            nc.vector.tensor_scalar(kb[:, 0:NT], kb[:, 0:NT], NEG_KEY, None, ALU.add).then_inc(c_ok, 1)
            for s in ST:
                nc.vector.memset(vaug[s][:], 0.0)
                nc.vector.memset(mrow[s][:], 0.0)
                nc.vector.memset(stack[s][:, :, :, :, DC:], 0.0).then_inc(kb_ok, 1)
            dve.wait_ge(kb_ok, 3)
            for s in ST:
                nc.vector.memset(vaug[s][:, :, :, DH:DH + 1], 1.0)
                nc.vector.memset(mrow[s][:, :, :, 0:1], 1.0)
                nc.vector.memset(stack[s][:, :, 0, :, DC:DC + 1], 1.0)
                nc.vector.memset(stack[s][:, :, 1, :, DC + 1:DC + 3], -1.0).then_inc(c_ok, 1)
            nc.vector.memset(ve[0][:], 1.0).then_inc(c_ok, 1)
            nc.vector.memset(ve[1][:], 1.0).then_inc(c_ok, 1)
            nc.vector.memset(rstd[0][:], 1.0).then_inc(c_ok, 1)
            dve.wait_ge(c_ok, 9)

        with nc.Block() as block:
            @block.sync
            def _(sp):
                sp.dma_start(eye[:], a["c_eye"]).then_inc(c_in, 16)
                sp.dma_start(maskf[:], a["c_masks"].rearrange("m p c -> p m c")).then_inc(c_in, 16)
                sp.dma_start(window[:], a["c_window"]).then_inc(c_in, 16)
                sp.dma_start(rope[:], a["c_rope"]).then_inc(c_in, 16)
                sp.dma_start(kb_i[:], a["mask"].rearrange("b (t p) -> p (b t)", p=P), allow_slow_non_contiguous=True).then_inc(c_in, 16)
                sp.dma_start(amc[:], am_d[0:B, :].rearrange("b (t p) -> p (b t)", p=P), allow_slow_non_contiguous=True).then_inc(c_in, 16)

                def load_h(it_in, s):
                    rows = hbuf[bass.ds(it_in * (NST * S) + s * S, S), :]
                    tok.inc(sp.dma_start(hcur[s][:], rows.rearrange("(t p) d -> p t d", p=P)), "h_in", s)

                def load_am(b, s):
                    tok.inc(sp.dma_start(amb[s][:], am_d[bass.ds(b, 1), :].to_broadcast([P, S])), "am_in", s)

                for dst, key in ((wqkv, "wqkv"), (wo, "wo"), (w1, "w1"), (w2, "w2"), (vec, "vec"), (b1, "b1")):
                    src = a[key][0] if key != "vec" else a[key][0:1].to_broadcast([P, VEC])
                    sp.dma_start(dst[:], src).then_inc(w_in, 16)
                for s in ST:
                    load_h(0, s)
                    load_am(s, s)
                with sp.Fori(0, L) as l:
                    with sp.Fori(0, PAIRS) as i:
                        it = l * PAIRS + i
                        for s in ST:
                            tok.wait(sp, "wam", s, it)
                            nxt = (i + 1) * NST + s
                            load_am(nxt, s)
                        for s in ST:
                            tok.wait(sp, "h_st", s, it, 0)
                            tok.wait(sp, "hb", s, it, 1)
                            tok.wait(sp, "hT_ps", s, it)
                            load_h(it + 1, s)
                        for s in ST:
                            tok.wait(sp, "h2", s, it)
                            rows = hbuf[bass.ds((it + PAIRS) * (NST * S) + s * S, S), :]
                            tok.inc(sp.dma_start(rows.rearrange("(t p) d -> p t d", p=P), hout[s][:]), "h_st", s)
                    for s in ST:
                        sp.wait_ge(tok.sem["h2"][s], l * PAIRS + (PAIRS + 1))
                    for dst, key in ((wqkv, "wqkv"), (wo, "wo"), (w1, "w1"), (w2, "w2"), (vec, "vec"), (b1, "b1")):
                        src = a[key][bass.ds(l + 1, 1)]
                        src = src.to_broadcast([P, VEC]) if key == "vec" else src.rearrange(
                            "o p n -> (o p) n" if key == "b1" else "o p c n -> (o p) c n")
                        sp.dma_start(dst[:], src).then_inc(w_in, 16)
                sp.wait_ge(w_in, 16 * 6 * (L + 1))
                for s in ST:
                    sp.wait_ge(tok.sem["h_st"][s], 16 * NIT + 1)
                    sp.wait_ge(tok.sem["h_in"][s], 16 * (NIT + 1))
                    sp.wait_ge(tok.sem["am_in"][s], 16 * (NIT + 1))

            @block.gpsimd
            def _(pool):
                nc.gpsimd.memset(half[:], -0.5).then_inc(half_ok, 1)
                pool.wait_ge(half_ok, 1)
                pool.wait_ge(c_ok, 9)
                with pool.Fori(0, L) as l:
                    wait_apart(pool, w_in, l * 96 + 96, w_in, 96)
                    with pool.Fori(0, PAIRS) as i:
                        it = l * PAIRS + i
                        for s in ST:
                            tok.wait(pool, "h_in", s, it)
                            tok.wait(pool, "h2", s, it, 0)
                            tok.inc(nc.gpsimd.tensor_tensor(resid[s][:], hcur[s][:], wide(BO), ALU.add), "hb", s)
                        for s in ST:
                            tok.wait(pool, "var1", s, it)
                            tok.inc(nc.gpsimd.tensor_tensor(rstd[s][:], ve[s][:], half[:], ALU.pow), "rstd1", s)
                        for s in ST:
                            tok.wait(pool, "h1", s, it)
                            tok.inc(nc.gpsimd.tensor_tensor(resid[s][:], h1[s][:], wide(B2), ALU.add), "hb", s)
                        for s in ST:
                            tok.wait(pool, "var2", s, it)
                            tok.inc(nc.gpsimd.tensor_tensor(rstd[s][:], ve[s][:], half[:], ALU.pow), "rstd2", s)

            @block.scalar
            def _(act):
                with act.Fori(0, L) as l:
                    wait_apart(act, w_in, l * 96 + 96, w_in, 96)
                    with act.Fori(0, PAIRS) as i:
                        it = l * PAIRS + i
                        attention_act(tok, act, it)
                        for f in range(FC):
                            for s in ST:
                                tok.wait(act, "w1_ps", s, it, f // 2 + 1)
                                hid = pT[s][:].rearrange("p a b -> p (a b)")
                                tok.inc(nc.scalar.activation(hid[:, f * S:(f + 1) * S],
                                                             bank[s][f // 2][:, (f % 2) * S:(f % 2 + 1) * S],
                                                             ACT.Gelu, bias=b1[:, f:f + 1]), "g", s)

            @block.vector
            def _(dve):
                setup_dve(dve)
                with dve.Fori(0, L) as l:
                    wait_apart(dve, w_in, l * 96 + 96, w_in, 96)
                    with dve.Fori(0, PAIRS) as i:
                        it = l * PAIRS + i
                        ch = Chain(tok, dve, it)

                        def col(s, am=False):
                            at = i * (NST * T) + s * T
                            return amc[:, bass.ds(at, T)] if am else kb[:, bass.ds(at, T)]
                        attention_dve(tok, ch, dve, it, col, BAND_COLS, True, False)
                        for s in ST:
                            tok.wait(dve, "wo_ps", s, it)
                            tok.wait(dve, "hb", s, it, 1)
                            ch.inc(nc.vector.tensor_tensor(h1[s][:].rearrange("p t d -> p (t d)"), bank[s][1][:, 0:2 * D],
                                                           resid[s][:].rearrange("p t d -> p (t d)"), ALU.add), s)
                        norm_dve(tok, ch, it, h1, h1, "1", (L1S, L1B, 1e-12, "h1"))
                        for s in ST:
                            tok.wait(dve, "w2_ps", s, it)
                            tok.wait(dve, "hb", s, it, 2)
                            tok.wait(dve, "h_st", s, it, 0)
                            ch.inc(nc.vector.tensor_tensor(hout[s][:].rearrange("p t d -> p (t d)"), bank[s][3][:, 0:2 * D],
                                                           resid[s][:].rearrange("p t d -> p (t d)"), ALU.add), s)
                        norm_dve(tok, ch, it, hout, hout, "2", (L2S, L2B, 1e-12, "h2"))
                        ch.end()

            @block.tensor
            def _(pe):
                pe.wait_ge(c_ok, 9)
                with pe.Fori(0, L) as l:
                    wait_apart(pe, w_in, l * 96 + 96, w_in, 96)
                    with pe.Fori(0, PAIRS) as i:
                        it = l * PAIRS + i
                        attention_pe(tok, pe, it, hcur, "h_in", h1, "h2", 0, BAND_COLS, BAND_COLS, True)
                        for s in ST:
                            tok.wait(pe, "h1T", s, it)
                            for f in range(FC):
                                for c in range(2):
                                    last = nc.tensor.matmul(bank[s][f // 2][:, (f % 2) * S:(f % 2 + 1) * S],
                                                            w1[:, c, f * P:(f + 1) * P], hT[s][:, c, :],
                                                            start=(c == 0), stop=(c == 1))
                                if f % 2:
                                    tok.inc(last, "w1_ps", s)
                        for s in ST:
                            tok.wait(pe, "g", s, it)
                            hid = pT[s][:].rearrange("p a b -> p (a b)")
                            for t in range(T):
                                for f in range(FC):
                                    last = nc.tensor.matmul(bank[s][3][:, t * D:(t + 1) * D],
                                                            hid[:, f * S + t * P:f * S + (t + 1) * P], w2[:, f, :],
                                                            start=(f == 0), stop=(f == FC - 1))
                            tok.inc(last, "w2_ps", s)

        layer_sems.close()
        car = Phase(sem, dict(
            common, x0=1, var0=1, rstd0=1, hb=1, lg_ps=1, ex=1, sig=1, sh_ps=3, sg=3, sh=3, sT_ps=1, sT=1,
            dn_ps=1, y=1, x_st=16, s_st=16, y_st=16, dve=CAUSAL_LINKS), "c", ("y", "sT", "s_st", "x_st", "y_st"))
        y_out = out.rearrange("b s d -> (b s) d")
        with nc.Block() as block:
            @block.sync
            def _(sp):
                sp.dma_start(gw[:], a["gw"]).then_inc(c_in, 16)

                def load_h(i, s):
                    rows = hbuf[bass.ds(i * (NST * S) + (L * N + s * S), S), :]
                    car.inc(sp.dma_start(hcur[s][:], rows.rearrange("(t p) d -> p t d", p=P)), "h_in", s)
                for s in ST:
                    load_h(0, s)
                with sp.Fori(0, PAIRS) as i:
                    for s in ST:
                        car.wait(sp, "h1", s, i)
                        car.wait(sp, "hb", s, i)
                        load_h(i + 1, s)
                    for s in ST:
                        rows = bass.ds(i * (NST * S) + s * S, S)
                        car.wait(sp, "sig", s, i)
                        car.inc(sp.dma_start(xs[rows, :].rearrange("(t p) d -> p t d", p=P), xr[s][:]), "x_st", s)
                        car.wait_apart(sp, "sT", s, i, None, c_in, 16 * 7)
                        car.inc(sp.dma_start(sd[:, rows], sT[s][:]), "s_st", s)
                    for s in ST:
                        rows = bass.ds(i * (NST * S) + s * S, S)
                        car.wait(sp, "y", s, i)
                        car.inc(sp.dma_start(y_out[rows, :].rearrange("(t p) d -> p t d", p=P), att[s][:]), "y_st", s)
                for s in ST:
                    for key, n in (("h_in", PAIRS + 1), ("x_st", PAIRS), ("s_st", PAIRS), ("y_st", PAIRS)):
                        sp.wait_ge(car.sem[key][s], 16 * n + (key in car.lifted))

            @block.gpsimd
            def _(pool):
                with pool.Fori(0, PAIRS) as i:
                    for s in ST:
                        car.wait(pool, "var0", s, i)
                        car.inc(nc.gpsimd.tensor_tensor(rstd[s][:], ve[s][:], half[:], ALU.pow), "rstd0", s)
                    for s in ST:
                        car.wait(pool, "y", s, i, 0)
                        car.inc(nc.gpsimd.tensor_tensor(resid[s][:], hcur[s][:], wide(BO), ALU.add), "hb", s)
                    for s in ST:
                        car.wait(pool, "var1", s, i)
                        car.inc(nc.gpsimd.tensor_tensor(rstd[s][:], ve[s][:], half[:], ALU.pow), "rstd1", s)

            @block.scalar
            def _(act):
                act.wait_ge(c_in, 16 * 7)
                with act.Fori(0, PAIRS) as i:
                    attention_act(car, act, i)
                    for s in ST:
                        car.wait(act, "lg_ps", s, i)
                        car.inc(nc.scalar.activation(sig[s][:], bank[s][3][:, 480:512].rearrange("p (t e) -> p t e", e=E),
                                                     ACT.Exp, scale=-1.0), "ex", s)
                    for f in range(FSC):
                        for s in ST:
                            hid = pT[s][:].rearrange("p a b -> p (a b)")
                            car.wait(act, "sh_ps", s, i, f + 1)
                            car.inc(nc.scalar.activation(hid[:, f * S:(f + 1) * S], bank[s][f][:, 0:S], ACT.Silu), "sg", s)
                    for s in ST:
                        car.wait(act, "sT_ps", s, i)
                        car.wait(act, "s_st", s, i, 0)
                        car.inc(nc.scalar.copy(sT[s][:], bank[s][0][0:E, 0:S]), "sT", s)

            @block.vector
            def _(dve):
                dve.wait_ge(c_in, 16 * 7)
                with dve.Fori(0, PAIRS) as i:
                    ch = Chain(car, dve, i)
                    for s in ST:
                        car.wait(dve, "h_in", s, i)
                    norm_dve(car, ch, i, hcur, h1, "0", (None, None, 1e-5, "x0"))

                    def col(s, am=False):
                        return kb[:, NT:NT + T]
                    for s in ST:
                        car.wait(dve, "y_st", s, i, 0)
                    attention_dve(car, ch, dve, i, col, CAUSAL_Q, False, True)
                    for s in ST:
                        car.wait(dve, "wo_ps", s, i)
                        car.wait(dve, "hb", s, i)
                        ch.inc(nc.vector.tensor_tensor(hout[s][:].rearrange("p t d -> p (t d)"), bank[s][1][:, 0:2 * D],
                                                       resid[s][:].rearrange("p t d -> p (t d)"), ALU.add), s)
                    for s in ST:
                        car.wait(dve, "x_st", s, i, 0)
                    norm_dve(car, ch, i, hout, [x[:, :, 0:D] for x in xr], "1", (None, None, 1e-5, "h1"))
                    for s in ST:
                        car.wait(dve, "ex", s, i)
                    ch.each(lambda s: nc.vector.tensor_scalar(sig[s][:], sig[s][:], 1.0, None, ALU.add))
                    for s in ST:
                        ch.wait(s)
                        car.inc(nc.vector.reciprocal(xr[s][:, :, D:XROW], sig[s][:]), "sig", s)
                    for f in range(FSC):
                        for s in ST:
                            hid = pT[s][:].rearrange("p a b -> p (a b)")
                            car.wait(dve, "sg", s, i, f + 1)
                            car.inc(nc.vector.tensor_tensor(hid[:, (FSC + f) * S:(FSC + f + 1) * S],
                                                            hid[:, f * S:(f + 1) * S], bank[s][f][:, S:2 * S], ALU.mult),
                                    "sh", s)
                    for s in ST:
                        car.wait(dve, "dn_ps", s, i)
                        car.inc(nc.vector.tensor_tensor(att[s][:].rearrange("p t d -> p (t d)"), bank[s][3][:, 0:2 * D],
                                                        hout[s][:].rearrange("p t d -> p (t d)"), ALU.add), "y", s)
                    ch.end()

            @block.tensor
            def _(pe):
                pe.wait_ge(c_in, 16 * 7)
                with pe.Fori(0, PAIRS) as i:
                    for s in ST:
                        car.wait(pe, "sT", s, i, 0)
                    attention_pe(car, pe, i, h1, "x0", xr, "y", 2, CAUSAL_Q, CAUSAL_K, False)
                    for s in ST:
                        car.wait(pe, "h1T", s, i)
                        for t in range(T):
                            for c in range(2):
                                last = nc.tensor.matmul(bank[s][3][:, 480 + t * E:480 + (t + 1) * E],
                                                        hT[s][:, c, t * P:(t + 1) * P], gw[:, c, :],
                                                        start=(c == 0), stop=(c == 1))
                        car.inc(last, "lg_ps", s)
                        for f in range(FSC):
                            for side in range(2):
                                for c in range(2):
                                    last = nc.tensor.matmul(bank[s][f][:, side * S:(side + 1) * S],
                                                            w1[:, c, side * FS + f * P:side * FS + (f + 1) * P],
                                                            hT[s][:, c, :], start=(c == 0), stop=(c == 1))
                            car.inc(last, "sh_ps", s)
                    for s in ST:
                        car.wait(pe, "sig", s, i)
                        car.wait(pe, "sh", s, i, 1)
                        for t in range(T):
                            last = nc.tensor.transpose(bank[s][0][0:E, t * P:(t + 1) * P], xr[s][:, t, D:XROW], eye[:])
                        car.inc(last, "sT_ps", s)
                    for s in ST:
                        car.wait(pe, "sh", s, i)
                        hid = pT[s][:].rearrange("p a b -> p (a b)")
                        for t in range(T):
                            for f in range(FSC):
                                last = nc.tensor.matmul(bank[s][3][:, t * D:(t + 1) * D],
                                                        hid[:, (FSC + f) * S + t * P:(FSC + f) * S + (t + 1) * P],
                                                        w2[:, f, :], start=(f == 0), stop=(f == FSC - 1))
                        car.inc(last, "dn_ps", s)


def choose(nc, a, sd, ids_d, N, CAP):
    SEG = P // E
    LEN = N // SEG
    NBLK = LEN // P
    NTILE = SEG * NBLK
    HI = CAP // 32
    with ExitStack() as ctx:
        sb = lambda name, shape, dt: ctx.enter_context(nc.sbuf_tensor("sel_" + name, shape, dt))
        sem = Semaphores(nc)
        sc = sb("sc", [P, LEN], F32)
        same = sb("same", [P, P], F32)
        before = sb("before", [P, P], F32)
        bits = sb("bits", [P, 30], I32)
        iota = sb("iota", [P, 32], F32)
        iotab = sb("iotab", [P, 32], BF16)
        partc = sb("partc", [P, 1], F32)
        tilec = sb("tilec", [P, NTILE], F32)
        tileb = sb("tileb", [P, NTILE], BF16)
        eye = sb("eye_c", [P, P], F32)
        thr = sb("thr", [P, 1], F32)
        cand = sb("cand", [P, 1], F32)
        cnt = sb("cnt", [P, 1], F32)
        flag = sb("flag", [P, 1], F32)
        junk = sb("junk", [P, LEN], F32)
        gt = sb("gt", [P, LEN], F32)
        eq = sb("eq", [P, LEN], F32)
        scan = sb("scan", [P, LEN], F32)
        ones = sb("ones", [P, LEN], F32)
        cnts = sb("cnts", [P, 4], F32)
        slot = sb("slot", [P, LEN], I32)
        part_i = sb("part_i", [P, LEN], I32)
        hilo = sb("hilo", [P, 2, LEN], F32)
        hlT = sb("hlT", [P, 2, NBLK, P], BF16)
        oh_hi = [sb(f"oh_hi{u}", [P, NTILE, 32], BF16) for u in range(2)]
        oh_lo = [sb(f"oh_lo{u}", [P, NTILE, 2, 32], BF16) for u in range(2)]
        ids_f = [sb(f"ids_f{u}", [32, 32], F32) for u in range(2)]
        ids_i = [sb(f"ids_i{u}", [32, 32], I32) for u in range(2)]
        ps_cnt = ctx.enter_context(nc.psum_tensor("ps_cnt", [P, 512], F32))
        ps_tr = [ctx.enter_context(nc.psum_tensor(f"ps_tr{u}", [P, 512], F32)) for u in range(2)]
        ps_id = [ctx.enter_context(nc.psum_tensor(f"ps_id{u}", [P, 512], F32)) for u in range(2)]
        tab_in, thr0, cand_ok, cnt_ok, tot_ok, flag_ok, thr_ok = (
            sem("s_tab"), sem("s_thr0"), sem("s_cand"), sem("s_cnt"), sem("s_tot"), sem("s_flag"), sem("s_thr"))
        if_ok = [sem(f"s_if{u}") for u in range(2)]
        chain, blk_in, blk_out, hl_ok, tr_ok, hlT_ok = (sem("s_chain"), sem("s_bin"), sem("s_bout"),
                                                        sem("s_hl"), sem("s_tr"), sem("s_hlT"))
        oh_ok, idp_ok, idi_ok, ids_st = ([sem(f"s_oh{u}") for u in range(2)], [sem(f"s_idp{u}") for u in range(2)],
                                         [sem(f"s_idi{u}") for u in range(2)], [sem(f"s_ids{u}") for u in range(2)])
        oc = [sem(f"s_oc{u}") for u in range(2)]
        ctx.callback(sem.close)
        sem.lift([thr_ok] + idp_ok + idi_ok + ids_st)
        block = ctx.enter_context(nc.Block())

        @block.sync
        def _(sp):
            sp.dma_start(sc[:], sd.rearrange("e (s n) -> (e s) n", n=LEN)).then_inc(tab_in, 16)
            for dst, key in ((same, "c_same"), (before, "c_before"), (bits, "c_bits"), (iota, "c_iota"),
                             (partc, "c_part"), (tilec, "c_tile"), (eye, "c_eye")):
                sp.dma_start(dst[:], a[key]).then_inc(tab_in, 16)
            with sp.Fori(0, E // 2) as i:
                for u in range(2):
                    sp.wait_ge(idi_ok[u], i + 2)
                    dst = ids_d[bass.ds(i * 2 + u, 1), :].rearrange("o (h l) -> (o h) l", l=32)
                    sp.dma_start(dst, ids_i[u][:]).then_inc(ids_st[u], 16)
            for u in range(2):
                sp.wait_ge(ids_st[u], 16 * (E // 2) + 1)

        @block.vector
        def _(dve):
            dve.wait_ge(tab_in, 16 * 8)
            nc.vector.memset(thr[:], 0.0)
            nc.vector.memset(ones[:], 1.0)
            nc.vector.tensor_copy(iotab[:], iota[:])
            nc.vector.tensor_copy(tileb[:], tilec[:]).then_inc(thr0, 1)
            dve.wait_ge(thr0, 1)
            with dve.Fori(0, 30) as k:
                dve.wait_ge(thr_ok, k + 1)
                nc.vector.tensor_tensor(cand[:].bitcast(I32), thr[:].bitcast(I32), bits[:, bass.ds(k, 1)],
                                        ALU.bitwise_or).then_inc(cand_ok, 1)
                dve.wait_ge(cand_ok, k + 1)
                nc.vector.tensor_scalar(junk[:], sc[:], cand[:], 0.0, ALU.is_ge, ALU.add,
                                        accum_out=cnt[:]).then_inc(cnt_ok, 1)
                dve.wait_ge(tot_ok, k + 1)
                nc.vector.tensor_scalar(flag[:], ps_cnt[:, 0:1], float(CAP), None, ALU.is_ge).then_inc(flag_ok, 1)
                dve.wait_ge(flag_ok, k + 1)
                nc.vector.scalar_tensor_tensor(out=thr[:], in0=cand[:], scalar=flag[:], in1=thr[:],
                                               op0=ALU.mult, op1=ALU.max).then_inc(thr_ok, 1)
            dve.wait_ge(thr_ok, 31)
            n = [0]

            def link(ins):
                n[0] += 1
                ins.then_inc(chain, 1)
                dve.wait_ge(chain, n[0])
            link(nc.vector.tensor_scalar(gt[:], sc[:], thr[:], 0.0, ALU.is_gt, ALU.add, accum_out=cnts[:, 0:1]))
            link(nc.vector.tensor_scalar(eq[:], sc[:], thr[:], 0.0, ALU.is_equal, ALU.add, accum_out=cnts[:, 1:2]))
            nc.vector.tensor_tensor_scan(scan[:], ones[:], eq[:], 0.0, ALU.mult, ALU.add).then_inc(blk_in, 1)
            dve.wait_ge(blk_out, 1)
            dve.wait_ge(blk_in, 1)
            link(nc.vector.tensor_copy(cnts[:, 0:2], ps_cnt[:, 0:2]))
            link(nc.vector.tensor_tensor(cnts[:, 2:3], cnts[:, 0:1], cnts[:, 1:2], ALU.add))
            link(nc.vector.tensor_scalar(cnts[:, 2:3], cnts[:, 2:3], -1.0, float(CAP), ALU.mult, ALU.add))
            link(nc.vector.tensor_scalar(scan[:], scan[:], cnts[:, 2:3], None, ALU.is_le))
            link(nc.vector.tensor_tensor(eq[:], eq[:], scan[:], ALU.mult))
            link(nc.vector.tensor_tensor(gt[:], gt[:], eq[:], ALU.add))
            link(nc.vector.tensor_tensor_scan(scan[:], ones[:], gt[:], 0.0, ALU.mult, ALU.add))
            nc.vector.tensor_copy(cnts[:, 3:4], scan[:, LEN - 1:LEN]).then_inc(blk_in, 1)
            dve.wait_ge(blk_out, 2)
            link(nc.vector.tensor_scalar(scan[:], scan[:], ps_cnt[:, 2:3], -2048.0, ALU.add, ALU.add))
            link(nc.vector.tensor_tensor(scan[:], scan[:], gt[:], ALU.mult))
            link(nc.vector.tensor_scalar(slot[:], scan[:], 2047.0, None, ALU.add))
            link(nc.vector.tensor_scalar(part_i[:], slot[:], 5, None, ALU.arith_shift_right))
            link(nc.vector.tensor_copy(hilo[:, 0, :], part_i[:]))
            link(nc.vector.tensor_scalar(part_i[:], slot[:], 31, None, ALU.bitwise_and))
            nc.vector.tensor_copy(hilo[:, 1, :], part_i[:]).then_inc(hl_ok, 1)
            for w in range(2):
                for c in range(NBLK // 4 if NBLK >= 4 else 1):
                    k = w * max(NBLK // 4, 1) + c
                    nb = min(4, NBLK)
                    dve.wait_ge(tr_ok, k + 1)
                    nc.vector.tensor_copy(hlT[:, w, c * 4:c * 4 + nb, :].rearrange("p c r -> p (c r)"),
                                          ps_tr[k % 2][:, 0:nb * P]).then_inc(hlT_ok, 1)
            dve.wait_ge(hlT_ok, 2 * max(NBLK // 4, 1))
            with dve.Fori(0, E // 2) as i:
                for u in range(2):
                    dve.wait_ge(idp_ok[u], i + 1)
                    rows = bass.ds((i * 2 + u) * SEG, SEG)
                    grid = [P, NBLK, SEG, 32]
                    lane = iotab[:].unsqueeze(1).unsqueeze(1).to_broadcast(grid)
                    hi = oh_hi[u][:].rearrange("p (c s) l -> p c s l", s=SEG)
                    lo = oh_lo[u][:].rearrange("p (c s) w l -> p c s w l", s=SEG)
                    nc.vector.tensor_tensor(hi, lane, hlT[:, 0, :, rows].unsqueeze(3).to_broadcast(grid), ALU.is_equal)
                    nc.vector.tensor_tensor(lo[:, :, :, 0, :], lane, hlT[:, 1, :, rows].unsqueeze(3).to_broadcast(grid),
                                            ALU.is_equal).then_inc(oc[u], 1)
                for u in range(2):
                    dve.wait_ge(oc[u], i * 2 + 1)
                    nc.vector.tensor_tensor(oh_lo[u][:, :, 1, :], oh_lo[u][:, :, 0, :],
                                            tileb[:].unsqueeze(2).to_broadcast([P, NTILE, 32]), ALU.mult).then_inc(oc[u], 1)
                    dve.wait_ge(oc[u], i * 2 + 2)
                    nc.vector.tensor_scalar(oh_lo[u][:, :, 0, :], oh_lo[u][:, :, 0, :], partc[:], None,
                                            ALU.mult).then_inc(oh_ok[u], 1)
                for u in range(2):
                    dve.wait_ge(idp_ok[u], i + 2)
                    nc.vector.tensor_copy(ids_f[u][:], ps_id[u][0:32, 0:32]).then_inc(if_ok[u], 1)
                for u in range(2):
                    dve.wait_ge(if_ok[u], i + 1)
                    dve.wait_ge(ids_st[u], i * 16 + 1)
                    nc.vector.scalar_tensor_tensor(out=ids_i[u][:], in0=ps_id[u][0:32, 32:64], scalar=float(P),
                                                   in1=ids_f[u][:], op0=ALU.mult, op1=ALU.add).then_inc(idi_ok[u], 1)

        @block.tensor
        def _(pe):
            pe.wait_ge(tab_in, 16 * 8)
            with pe.Fori(0, 30) as k:
                pe.wait_ge(cnt_ok, k + 1)
                nc.tensor.matmul(ps_cnt[:, 0:1], same[:], cnt[:], start=True, stop=True).then_inc(tot_ok, 1)
            pe.wait_ge(blk_in, 1)
            pe.wait_ge(chain, 2)
            pe.wait_ge(thr_ok, 31)
            nc.tensor.matmul(ps_cnt[:, 0:1], same[:], cnts[:, 0:1], start=True, stop=True)
            nc.tensor.matmul(ps_cnt[:, 1:2], before[:], cnts[:, 1:2], start=True, stop=True).then_inc(blk_out, 1)
            pe.wait_ge(blk_in, 2)
            nc.tensor.matmul(ps_cnt[:, 2:3], before[:], cnts[:, 3:4], start=True, stop=True).then_inc(blk_out, 1)
            pe.wait_ge(hl_ok, 1)
            nf = max(NBLK // 4, 1)
            for w in range(2):
                for c in range(nf):
                    k = w * nf + c
                    if k >= 2:
                        pe.wait_ge(hlT_ok, k - 1)
                    for j in range(min(4, NBLK)):
                        blk = c * 4 + j
                        last = nc.tensor.transpose(ps_tr[k % 2][:, j * P:(j + 1) * P],
                                                   hilo[:, w, blk * P:(blk + 1) * P], eye[:])
                    last.then_inc(tr_ok, 1)
            with pe.Fori(0, E // 2) as i:
                for u in range(2):
                    pe.wait_ge(oh_ok[u], i + 1)
                    pe.wait_ge(idi_ok[u], i + 1)
                    for t in range(NTILE):
                        last = nc.tensor.matmul(ps_id[u][0:32, 0:64], oh_hi[u][:, t, :],
                                                oh_lo[u][:, t].rearrange("p w l -> p (w l)"),
                                                start=(t == 0), stop=(t == NTILE - 1))
                    last.then_inc(idp_ok[u], 1)


def experts(nc, a, xs, ids_d, out, N, CAP):
    G = CAP // P
    HALF = 512
    NHALF = CAP // HALF
    y_out = out.rearrange("b s d -> (b s) d")
    U = (0, 1)
    with ExitStack() as ctx:
        sb = lambda name, shape, dt: ctx.enter_context(nc.sbuf_tensor("exp_" + name, shape, dt))
        sem = Semaphores(nc)
        eye = sb("eye_x", [P, P], F32)
        wg = [sb(f"wg{u}", [DC, 2, FF], F32) for u in U]
        wu = [sb(f"wu{u}", [DC, 2, FF], F32) for u in U]
        wd = [sb(f"wd{u}", [P, FC, D], F32) for u in U]
        idx = [sb(f"idx{u}", [P, G], I32) for u in U]
        xg = [sb(f"xg{u}", [P, G, XROW], F32) for u in U]
        xT = sb("xT", [DC, 2, CAP], F32)
        hid = sb("hid", [P, NHALF, FC, HALF], F32)
        sg = [sb(f"sg{u}", [P, HALF], F32) for u in U]
        yb = [sb(f"yb{u}", [P, G, D], F32) for u in U]
        ps_x = [ctx.enter_context(nc.psum_tensor(f"ps_x{i}", [P, 512], F32)) for i in range(2)]
        ps_g = [ctx.enter_context(nc.psum_tensor(f"ps_g{i}", [P, 512], F32)) for i in range(2)]
        ps_u = [ctx.enter_context(nc.psum_tensor(f"ps_u{i}", [P, 512], F32)) for i in range(2)]
        ps_y = [ctx.enter_context(nc.psum_tensor(f"ps_y{i}", [P, 512], F32)) for i in range(2)]
        eye_in = sem("x_eye")
        w_in = [sem(f"x_w{u}") for u in U]
        i_in = [sem(f"x_i{u}") for u in U]
        g_in = [sem(f"x_g{u}") for u in U]
        xT_ps, xT_v, xT_s, gu_ps, sg_ok, hid_ok, y_ps, y_ok = (sem("x_xTp"), sem("x_xTv"), sem("x_xTs"), sem("x_gup"),
                                                                sem("x_sg"), sem("x_hid"), sem("x_yp"), sem("x_y"))
        y_st = sem("x_yst")
        NX = G // 2
        NF = NHALF * FC
        ctx.callback(sem.close)
        sem.lift([y_ok, hid_ok])
        block = ctx.enter_context(nc.Block())

        @block.sync
        def _(sp):
            sp.dma_start(eye[:], a["c_eye"]).then_inc(eye_in, 16)

            def load(e, u):
                one = bass.ds(e, 1)
                sp.dma_start(idx[u][:], ids_d[one, :].rearrange("o (p g) -> (o p) g", g=G)).then_inc(i_in[u], 16)
                for dst, key in ((wg, "ewg"), (wu, "ewu"), (wd, "ewd")):
                    sp.dma_start(dst[u][:], a[key][one].rearrange("o p c n -> (o p) c n")).then_inc(w_in[u], 16)
            for u in U:
                load(u, u)
            with sp.Fori(0, E // 2 - 1) as i:
                for u in U:
                    sp.wait_ge(y_st, (i * 2 + u + 1) * (16 * G))
                    load(i * 2 + u + 2, u)
            sp.wait_ge(y_st, 16 * G * E)

        @block.gpsimd
        def _(pool):
            def gather(i, u):
                wait_apart(pool, i_in[u], i * 16 + 16, eye_in, 16)
                for g in range(G):
                    pool.indirect_dma_start(xg[u][:, g, :], None, xs,
                                            bass.IndirectOffsetOnAxis(ap=idx[u][:, g:g + 1], axis=0)
                                            ).then_inc(g_in[u], 16)

            def scatter(i, u):
                if not (isinstance(i, int) and i * 2 + u == 0):
                    pool.wait_ge(y_st, (i * 2 + u) * (16 * G))
                for g in range(G):
                    if g % 2 == 0:
                        wait_apart(pool, y_ok, (i * 2 + u) * NX + (g // 2 + 2), eye_in, 16)
                    pool.indirect_dma_start(y_out, bass.IndirectOffsetOnAxis(ap=idx[u][:, g:g + 1], axis=0),
                                            yb[u][:, g, :], None, compute_op=ALU.add).then_inc(y_st, 16)
            pool.wait_ge(eye_in, 16)
            gather(0, 0)
            gather(0, 1)
            for u in U:
                scatter(0, u)
                gather(1, u)
            with pool.Fori(1, E // 2 - 1) as i:
                for u in U:
                    scatter(i, u)
                    gather(i + 1, u)
            for u in U:
                scatter(E // 2 - 1, u)

        @block.scalar
        def _(act):
            with act.Fori(0, E // 2) as i:
                for u in U:
                    e = i * 2 + u
                    for k in range(1, NX, 2):
                        act.wait_ge(xT_ps, e * NX + k + 1)
                        nc.scalar.copy(xT[:, :, k * 2 * P:(k + 1) * 2 * P], ps_x[k % 2][0:DC, :].rearrange("p (c n) -> p c n", c=2)
                                       ).then_inc(xT_s, 1)
                    for k in range(NF):
                        act.wait_ge(gu_ps, e * NF + k + 1)
                        act.wait_ge(hid_ok, e * NF + max(k, 1))
                        nc.scalar.activation(sg[k % 2][:], ps_g[k % 2][:], ACT.Silu).then_inc(sg_ok, 1)

        @block.vector
        def _(dve):
            with dve.Fori(0, E // 2) as i:
                for u in U:
                    e = i * 2 + u
                    for k in range(0, NX, 2):
                        dve.wait_ge(xT_ps, e * NX + k + 1)
                        nc.vector.tensor_copy(xT[:, :, k * 2 * P:(k + 1) * 2 * P],
                                              ps_x[k % 2][0:DC, :].rearrange("p (c n) -> p c n", c=2)).then_inc(xT_v, 1)
                    for k in range(NF):
                        dve.wait_ge(sg_ok, e * NF + k + 1)
                        nc.vector.tensor_tensor(hid[:, k // FC, k % FC, :], sg[k % 2][:], ps_u[k % 2][:], ALU.mult
                                                ).then_inc(hid_ok, 1)
                    for k in range(NX):
                        dve.wait_ge(y_ps, e * NX + k + 1)
                        for j in range(2):
                            g = 2 * k + j
                            last = nc.vector.tensor_scalar(yb[u][:, g, :], ps_y[k % 2][:, j * D:(j + 1) * D],
                                                           xg[u][:, g, bass.ds(e + D, 1)], None, ALU.mult)
                        last.then_inc(y_ok, 1)

        @block.tensor
        def _(pe):
            pe.wait_ge(eye_in, 16)
            with pe.Fori(0, E // 2) as i:
                for u in U:
                    e = i * 2 + u
                    pe.wait_ge(g_in[u], i * (16 * G) + 16 * G)
                    for k in range(NX):
                        if k >= 2:
                            pe.wait_ge(xT_s if k % 2 else xT_v, e * (NX // 2) + k // 2)
                        for c in range(2):
                            for j in range(2):
                                last = nc.tensor.transpose(ps_x[k % 2][0:DC, c * 2 * P + j * P:c * 2 * P + (j + 1) * P],
                                                           xg[u][:, 2 * k + j, c * DC:(c + 1) * DC], eye[:])
                        last.then_inc(xT_ps, 1)
                    pe.wait_ge(xT_v, (e + 1) * (NX // 2))
                    pe.wait_ge(xT_s, (e + 1) * (NX // 2))
                    pe.wait_ge(w_in[u], i * 48 + 48)
                    for k in range(NF):
                        n0, f = (k // FC) * HALF, k % FC
                        pe.wait_ge(hid_ok, e * NF + max(k, 1))
                        for w, dst in ((wg, ps_g), (wu, ps_u)):
                            for c in range(2):
                                last = nc.tensor.matmul(dst[k % 2][:], w[u][:, c, f * P:(f + 1) * P],
                                                        xT[:, c, n0:n0 + HALF], start=(c == 0), stop=(c == 1))
                        last.then_inc(gu_ps, 1)
                    pe.wait_ge(hid_ok, e * NF + (NF + 1))
                    for k in range(NX):
                        pe.wait_ge(y_ok, e * NX + max(k, 1))
                        for j in range(2):
                            g = 2 * k + j
                            n0, o = g * P // HALF, g * P % HALF
                            for f in range(FC):
                                last = nc.tensor.matmul(ps_y[k % 2][:, j * D:(j + 1) * D], hid[:, n0, f, o:o + P],
                                                        wd[u][:, f, :], start=(f == 0), stop=(f == FC - 1))
                        last.then_inc(y_ps, 1)


def kernel(**inputs):
    import concourse.bacc as bacc
    from concourse.bass_utils import run_bass_kernel_spmd

    g = {k: np.asarray(v) for k, v in inputs.items()}
    tok = {k[len("L0_tok_"):]: v for k, v in g.items() if k.startswith("L0_tok_")}
    B = g["x"].shape[0]
    L = tok["Wq"].shape[0]
    V = tok["emb_word"].shape[0]
    chunks = lambda w, p: np.swapaxes(w.reshape(w.shape[:-2] + (w.shape[-2] // p, p, w.shape[-1])), -3, -2)
    tr = lambda w: np.swapaxes(w, -1, -2)
    z = lambda n: np.zeros(n, np.float32)
    one = lambda w: w[None]
    wqkv = np.concatenate([np.concatenate([tok["Wq"], tok["Wk"], tok["Wv"]], -1), one(g["L0_attn_W_attn"])])
    wo = np.concatenate([tok["Wo"], one(g["L0_attn_W_proj"])])
    w1 = np.concatenate([tok["W1"], one(np.concatenate([tr(g["L0_ffn_Ws_g"]), tr(g["L0_ffn_Ws_u"])], -1))])
    w2 = np.concatenate([tok["W2"], one(np.concatenate([tr(g["L0_ffn_Ws_d"]), z((FF - FS, D))]))])
    vec = np.concatenate([
        np.concatenate([tok[k] for k in ("bq", "bk", "bv", "bo", "ln1_s", "ln1_b", "b2", "ln2_s", "ln2_b")], -1),
        one(np.concatenate([g["L0_attn_b_attn"], g["L0_attn_b_proj"], z(5 * D)]))])
    b1 = np.concatenate([tok["b1"], z((1, FF))]).reshape(L + 1, FC, P)
    arrays = {
        "x": g["x"], "mask": g["mask_BS_i1_0"], "emb_word": tok["emb_word"], "emb_pos": tok["emb_pos"][:S],
        "emb_ln": one(np.concatenate([tok["emb_ln_s"], tok["emb_ln_b"]])),
        "wqkv": chunks(wqkv, DC), "wo": chunks(wo, DC), "w1": chunks(w1, DC), "w2": chunks(w2, P), "vec": vec,
        "b1": tr(b1), "gw": chunks(tr(g["L0_ffn_gate_weight"]), DC), "ewg": chunks(tr(g["L0_ffn_Wg"]), DC),
        "ewu": chunks(tr(g["L0_ffn_Wu"]), DC), "ewd": chunks(tr(g["L0_ffn_Wd"]), P),
    }
    arrays.update(constants())
    arrays.update(select_constants(B * S, P // E))
    nc = bacc.Bacc("TRN2", target_bir_lowering=False, num_devices=1)
    feed, aps = {}, {}
    for name, v in arrays.items():
        v = np.ascontiguousarray(v)
        feed[f"in_{name}"] = v
        aps[name] = nc.dram_tensor(f"in_{name}", list(v.shape), mybir.dt.from_np(v.dtype), kind="ExternalInput").ap()
    out = nc.dram_tensor("out", [B, S, D], F32, kind="ExternalOutput").ap()
    build(nc, aps, out, B, L, V)
    r = run_bass_kernel_spmd(nc, [feed], core_ids=[0])
    return r.results[0]["out"]
```

```python
import numpy as np
import concourse.bass as bass
from concourse import mybir
from collections import namedtuple
from contextlib import ExitStack

F32 = mybir.dt.float32
BF16 = mybir.dt.bfloat16
I32 = mybir.dt.int32
ALU = mybir.AluOpType
ACT = mybir.ActivationFunctionType
AX = mybir.AxisListType.X

P = 128
D = 192
DC = 96
NH = 12
DH = 16
S = 256
W = 64
T = S // P
FF = 768
FC = FF // P
FS = 384
FSC = FS // P
E = 16
NST = 2
SLOTS = 6
STK = P
XROW = D + E
NEG_BAND = -1.0e30
NEG_KEY = -1.0e30
M_FLOOR = -4.0e9
SCALE = 0.25
ST = (0, 1)

BAND_COLS = [(0, 0, 192), (192, 64, 192)]
CAUSAL_Q = [(0, 0, 128), (128, 0, 256)]
CAUSAL_K = [(0, 0, 256), (256, 128, 128)]
SCOLS = 384

TOK_FRONT_LINKS = 5
TOK_BACK_LINKS = 10
CAUSAL_FRONT_LINKS = 9
CAUSAL_BACK_LINKS = 6

Turn = namedtuple("Turn", "s it pair wf wb")

Plan = namedtuple("Plan", "input qk proj v h1 up res stats mean center norm")
TOK_PLAN = Plan(input=1, qk=3, proj=2, v=6, h1=8, up=9, res=1, stats=2, mean=2, center=3, norm=4)
CAUSAL_PLAN = Plan(input=0, qk=1, proj=2, v=12, h1=10, up=12, res=2, stats=3, mean=4, center=5, norm=6)
LAG = 2


def constants():
    def cols(ranges, fn):
        m = np.zeros((P, SCOLS), np.float32)
        for t, (c, f0, w) in enumerate(ranges):
            part = (t * P + np.arange(P))[:, None]
            free = (f0 + np.arange(w))[None, :]
            m[:, c:c + w] = fn(part, free)
        return m

    band = lambda a, b: np.where(np.abs(a - b) <= W, 0.0, NEG_BAND)
    masks = np.stack([
        cols(BAND_COLS, band),
        cols(BAND_COLS, band),
        cols(CAUSAL_Q, lambda q, k: np.where(k <= q, 0.0, NEG_BAND)),
        cols(CAUSAL_K, lambda k, q: np.where(k <= q, 0.0, NEG_BAND)),
    ]).astype(np.float32)
    k = (np.arange(T)[None, :] * P + np.arange(P)[:, None])[:, :, None]
    q = np.arange(S)[None, None, :]
    window = (np.abs(k // W - q // W) <= 1).astype(np.float32) / (3 * W)
    inv = (1.0 / 10000.0 ** (np.arange(0, DH, 2, dtype=np.float32) / DH)).astype(np.float32)
    fr = np.arange(S, dtype=np.float32)[:, None] * inv[None, :]
    cos, sin = np.cos(fr).astype(np.float32), np.sin(fr).astype(np.float32)
    rope = np.zeros((P, T, 3, DH), np.float32)
    for t in range(T):
        rope[:, t, 0] = np.repeat(cos[t * P:(t + 1) * P], 2, axis=1)
        rope[:, t, 1, 0:8] = -sin[t * P:(t + 1) * P]
        rope[:, t, 2, 0:8] = sin[t * P:(t + 1) * P]
    return {"c_eye": np.eye(P, dtype=np.float32), "c_masks": masks, "c_window": window, "c_rope": rope}


def select_constants(n, seg):
    r = np.arange(P)
    same = (r[:, None] // seg == r[None, :] // seg)
    before = same & (r[:, None] < r[None, :])
    nblk = n // seg // P
    tile = (np.arange(seg)[None, :] * nblk + np.arange(nblk)[:, None]).astype(np.float32)
    bits = (1 << np.arange(29, -1, -1)).astype(np.int32)
    return {
        "c_same": same.astype(np.float32), "c_before": before.astype(np.float32),
        "c_bits": np.broadcast_to(bits[None], (P, 30)).copy(),
        "c_iota": np.broadcast_to(np.arange(32, dtype=np.float32)[None], (P, 32)).copy(),
        "c_part": np.arange(P, dtype=np.float32)[:, None].copy(),
        "c_tile": np.broadcast_to(tile.reshape(1, -1), (P, seg * nblk)).copy(),
    }


def wait_apart(eng, sem, value, held, held_value):
    eng.lower_val(value)
    eng.wait_ge(held, held_value)
    eng.wait_ge(sem, value)


class Semaphores:

    def __init__(self, nc):
        self.nc, self.all = nc, []

    def __call__(self, name):
        self.all.append(self.nc.alloc_semaphore(name))
        return self.all[-1]

    def lift(self, sems):
        for s in sems:
            self.nc.sync.sem_inc(s, 1)
        self.nc.all_engine_barrier()

    def close(self):
        self.nc.clear_and_free_semaphores(self.all)
        self.nc.all_engine_barrier()
        self.all = []


class Phase:

    def __init__(self, sems, counts, tag, lifted):
        self.n, self.lifted = counts, lifted
        self.sem = {k: [sems(f"{tag}_{k}{s}") for s in ST] for k in counts}
        sems.lift([x for k in lifted for x in self.sem[k]])

    def value(self, key, it, k=None):
        n = self.n[key]
        return it * n + ((n if k is None else k) + (key in self.lifted))

    def wait(self, eng, key, s, it, k=None):
        assert k != 0 or key in self.lifted, key
        eng.wait_ge(self.sem[key][s], self.value(key, it, k))

    def wait_apart(self, eng, key, s, it, k, held, held_value):
        wait_apart(eng, self.sem[key][s], self.value(key, it, k), held, held_value)

    def inc(self, ins, key, s):
        ins.then_inc(self.sem[key][s], 16 if key in ("h_in", "am_in", "h_st", "x_st", "y_st", "s_st") else 1)


def build(nc, a, out, B, L, V):
    ctx = ExitStack()
    with ctx:
        N = B * S
        NT = N // P
        PAIRS = B // NST
        NIT = L * PAIRS
        CAP = N // E * 2
        hbuf = nc.dram_tensor("hbuf", [(L + 1) * N + NST * S, D], F32, kind="Internal").ap()
        xs = nc.dram_tensor("xs", [N, XROW], F32, kind="Internal").ap()
        sd = nc.dram_tensor("sd", [E, N], F32, kind="Internal").ap()
        am_d = nc.dram_tensor("am_d", [B + NST, S], F32, kind="Internal").ap()
        ids_d = nc.dram_tensor("ids_d", [E, CAP], I32, kind="Internal").ap()
        embed(nc, a, hbuf, am_d, B, V, (L + 1) * N)
        tower(nc, a, hbuf, am_d, xs, sd, out, B, L)
        choose(nc, a, sd, ids_d, N, CAP)
        experts(nc, a, xs, ids_d, out, N, CAP)


def embed(nc, a, hbuf, am_d, B, V, HROWS):
    N = B * S
    NT = N // P
    G = 4
    STEPS = NT // G
    PAST = 2
    MASK_LINKS = 15
    with ExitStack() as ctx:
        sb = lambda name, shape, dt: ctx.enter_context(nc.sbuf_tensor("emb_" + name, shape, dt))
        sem = Semaphores(nc)
        ids_raw = sb("ids_raw", [P, NT], I32)
        idf = sb("idf", [P, NT], F32)
        neg = sb("neg", [P, NT], F32)
        ids = sb("ids", [P, NT], I32)
        emb = sb("emb", [P, NT, D], F32)
        pos = sb("pos", [P, T, D], F32)
        lnw = sb("lnw", [P, 2 * D], F32)
        st = [sb(f"st{u}", [P, G, 6], F32) for u in range(2)]
        mv = [sb(f"mv{u}", [P, G, 2], F32) for u in range(2)]
        ve = [sb(f"ve{u}", [P, G], F32) for u in range(2)]
        half = sb("half", [P, G], F32)
        rstd = [sb(f"rstd{u}", [P, G], F32) for u in range(2)]
        z = [sb(f"z{u}", [P, G, D], F32) for u in range(2)]
        mi = sb("mi", [B, S], I32)
        PADW = S + 2 * W
        mw = [sb("mw0", [B, PADW], F32), sb("mw1", [B, PADW], F32)]
        in_sem, row_sem, mask_sem, am_st = sem("e_in"), sem("e_row"), sem("e_mask"), sem("e_amst")
        ids_ok, gathered = sem("e_ids"), [sem(f"e_gath{g}") for g in range(STEPS)]
        chain, var_ok, rstd_ok, z_ok, z_out, const_ok = (sem("e_chain"), sem("e_var"), sem("e_rstd"), sem("e_z"),
                                                         [sem(f"e_zout{u}") for u in range(2)], sem("e_const"))
        ctx.callback(sem.close)
        block = ctx.enter_context(nc.Block())

        @block.sync
        def _(sp):
            sp.dma_start(ids_raw[:], a["x"].rearrange("b (t p) -> p (b t)", p=P), allow_slow_non_contiguous=True).then_inc(in_sem, 16)
            sp.dma_start(pos[:], a["emb_pos"].rearrange("(t p) d -> p t d", p=P)).then_inc(row_sem, 16)
            sp.dma_start(lnw[:], a["emb_ln"].to_broadcast([P, 2 * D])).then_inc(row_sem, 16)
            sp.dma_start(mi[:], a["mask"]).then_inc(mask_sem, 16)
            sp.wait_ge(chain, MASK_LINKS)
            sp.dma_start(am_d[0:B, :], mw[0][:, 0:S]).then_inc(am_st, 16)
            sp.dma_start(am_d[B:B + NST, :], mw[0][0:NST, 0:S]).then_inc(am_st, 16)
            for g in range(STEPS):
                sp.wait_ge(z_ok, g + 1)
                rows = hbuf[g * G * P:(g + 1) * G * P, :]
                sp.dma_start(rows.rearrange("(t p) d -> p t d", p=P), z[g % 2][:]).then_inc(z_out[g % 2], 16)
                if g == 0:
                    rows = hbuf[HROWS:HROWS + G * P, :]
                    sp.dma_start(rows.rearrange("(t p) d -> p t d", p=P), z[0][:]).then_inc(z_out[0], 16)
            for u in range(2):
                sp.wait_ge(z_out[u], 16 * (STEPS // 2 + (u == 0)))
            sp.wait_ge(am_st, 32)

        @block.gpsimd
        def _(pool):
            nc.gpsimd.memset(half[:], -0.5).then_inc(const_ok, 1)
            pool.wait_ge(ids_ok, 1)
            for g in range(STEPS + PAST):
                if g < STEPS:
                    for t in range(g * G, (g + 1) * G):
                        pool.indirect_dma_start(emb[:, t, :], None, a["emb_word"],
                                                bass.IndirectOffsetOnAxis(ap=ids[:, t:t + 1], axis=0)
                                                ).then_inc(gathered[g], 16)
                if g == PAST:
                    pool.wait_ge(const_ok, 1)
                if g >= PAST:
                    u = (g - PAST) % 2
                    pool.wait_ge(var_ok, g - PAST + 1)
                    nc.gpsimd.tensor_tensor(rstd[u][:], ve[u][:], half[:], ALU.pow).then_inc(rstd_ok, 1)

        @block.vector
        def _(dve):
            n = [0]

            def link(ins):
                n[0] += 1
                ins.then_inc(chain, 1)
                dve.wait_ge(chain, n[0])

            dve.wait_ge(in_sem, 16)
            link(nc.vector.tensor_copy(idf[:], ids_raw[:]))
            link(nc.vector.tensor_scalar(neg[:], idf[:], 0.0, float(V), ALU.is_lt, ALU.mult))
            link(nc.vector.tensor_tensor(idf[:], idf[:], neg[:], ALU.add))
            link(nc.vector.tensor_scalar(idf[:], idf[:], 0.0, float(V - 1), ALU.max, ALU.min))
            nc.vector.tensor_copy(ids[:], idf[:]).then_inc(ids_ok, 1)
            link(nc.vector.memset(mw[0][:], 0.0))
            dve.wait_ge(mask_sem, 16)
            link(nc.vector.tensor_scalar(mw[0][:, W:W + S], mi[:], 0, None, ALU.is_gt))
            src = 0
            for sh in (1, 2, 4, 8, 16, 32, 64):
                width = PADW - sh
                nc.vector.tensor_copy(mw[1 - src][:, width:PADW], mw[src][:, width:PADW])
                link(nc.vector.tensor_tensor(mw[1 - src][:, 0:width], mw[src][:, 0:width],
                                             mw[src][:, sh:sh + width], ALU.max))
                src = 1 - src
            link(nc.vector.tensor_tensor(mw[0][:, 0:S], mw[1][:, 0:S], mw[1][:, 1:S + 1], ALU.max))
            link(nc.vector.tensor_scalar(mw[0][:, 0:S], mw[0][:, 0:S], -1.0, 1.0, ALU.mult, ALU.add))
            assert n[0] == MASK_LINKS, n
            dve.wait_ge(row_sem, 32)

            def moments(g):
                u, e = g % 2, emb[:, g * G:(g + 1) * G, :]
                e4 = e.rearrange("p (c t) d -> p c t d", t=T)
                dve.wait_ge(gathered[g], 16 * G)
                link(nc.vector.tensor_tensor(e4, e4, pos[:].unsqueeze(1).to_broadcast([P, G // T, T, D]), ALU.add))
                for t in range(G):
                    last = nc.vector.bn_stats(st[u][:, t, :], e[:, t, :])
                link(last)
                for t in range(G):
                    last = nc.vector.bn_aggr(mv[u][:, t, :], st[u][:, t, :])
                link(last)
                nc.vector.tensor_scalar(ve[u][:], mv[u][:, :, 1], 1e-12, None, ALU.add).then_inc(var_ok, 1)

            def normalise(g):
                u, e = g % 2, emb[:, g * G:(g + 1) * G, :]
                for t in range(G):
                    last = nc.vector.scalar_tensor_tensor(e[:, t, :], e[:, t, :], mv[u][:, t, 0:1], lnw[:, 0:D],
                                                          ALU.subtract, ALU.mult)
                link(last)
                dve.wait_ge(rstd_ok, g + 1)
                if g >= 2:
                    dve.wait_ge(z_out[u], 16 * (g // 2 + (u == 0)))
                for t in range(G):
                    last = nc.vector.scalar_tensor_tensor(z[u][:, t, :], e[:, t, :], rstd[u][:, t:t + 1], lnw[:, D:2 * D],
                                                          ALU.mult, ALU.add)
                last.then_inc(z_ok, 1)

            moments(0)
            for g in range(STEPS):
                if g + 1 < STEPS:
                    moments(g + 1)
                normalise(g)


def tower(nc, a, hbuf, am_d, xs, sd, out, B, L):
    N = B * S
    NT = N // P
    PAIRS = B // NST
    NIT = L * PAIRS
    with ExitStack() as ctx:
        sb = lambda name, shape, dt: ctx.enter_context(nc.sbuf_tensor(name, shape, dt))
        sbs = lambda name, shape, dt: [sb(f"{name}{s}", shape, dt) for s in ST]
        sem = Semaphores(nc)

        bank = [[ctx.enter_context(nc.psum_tensor(f"bank{s}{i}", [P, 512], F32)) for i in range(4)] for s in ST]

        wqkv = sb("wqkv", [DC, 2, 3 * D], F32)
        wo = sb("wo", [DC, 2, D], F32)
        w1 = sb("w1", [DC, 2, FF], F32)
        w2 = sb("w2", [P, FC, D], F32)
        vecf = sb("vecf", [P, 4 * D], F32)
        vec = sb("vec", [P, 5 * D], F32)
        b1 = sb("b1", [P, FC], F32)
        BO = 3 * D
        L1S, L1B, B2, L2S, L2B = (i * D for i in range(5))
        wide = lambda at: vec[:, at:at + D].unsqueeze(1).to_broadcast([P, T, D])

        eye = sb("eye", [P, P], F32)
        eyeb = sb("eyeb", [P, P], BF16)
        maskf = sb("maskf", [P, 4, SCOLS], F32)
        maskb = sb("maskb", [P, 4, SCOLS], BF16)
        window = sb("window", [P, T, S], F32)
        rope = sb("rope", [P, T, 3, DH], F32)
        kb_i = sb("kb_i", [P, NT], I32)
        kb = sb("kb", [P, NT + 2 * NST * T], F32)
        amc = sb("amc", [P, NT], F32)
        half = sb("half", [P, T], F32)

        hcur = sbs("hcur", [P, T, D], F32)
        hT = sbs("hT", [DC, 2, S], F32)
        qk = sbs("qk", [P, T, 2, NH, DH], F32)
        rem = sbs("rem", [P, T, 2, NH, DH], F32)
        vaug = sbs("vaug", [P, T, NH, 32], F32)
        stack = sbs("stack", [P, T, 2, NH, STK], BF16)
        qT = sbs("qT", [P, NH, S], BF16)
        kT = sbs("kT", [P, NH, S], BF16)
        mx = sbs("mx", [P, T, NH], F32)
        mrow = sbs("mrow", [P, T, NH, 32], BF16)
        NPT = 4
        pT = sbs("pT", [P, NPT, SCOLS], F32)
        amb = sbs("amb", [P, S], F32)
        wam = sbs("wam", [P, T, S], F32)
        den = sbs("den", [P, T, NH], F32)
        att = sbs("att", [P, T, D], F32)
        resid = sbs("resid", [P, T, D], F32)
        h1 = sbs("h1", [P, T, D], F32)
        hout = sbs("hout", [P, T, D], F32)
        stt = sbs("stt", [P, T, 6], F32)
        mv = sbs("mv", [P, T, 2], F32)
        ve = sbs("ve", [P, T], F32)
        rstd = sbs("rstd", [P, T], F32)
        gw = sb("gw", [DC, 2, E], F32)
        xr = sbs("xr", [P, T, XROW], F32)
        sig = sbs("sig", [P, T, E], F32)
        sT = sbs("sT", [E, S], F32)

        w_front, w_back = sem("w_front"), sem("w_back")
        c_in, c_ok, kb_ok, half_ok = sem("c_in"), sem("c_ok"), sem("kb_ok"), sem("half_ok")

        common = dict(
            h_in=16, hT_ps=1, hT=1, qk_ps=2, v_ps=1, qk=2, v=1, stk=1, fill=6, ev_v=3, ev_s=3,
            sc1=NH, mx=NH, m=1, mT_ps=3, mT=3, sc2=NH, p=NH, pv=NH, ot=1, otT_ps=2, att=1,
            aT_ps=1, aT=1, wo_ps=1, var1=1, rstd1=1, h1=1, h1T_ps=1, h1T=1)
        ctx.callback(sem.close)
        layer_sems = Semaphores(nc)
        tok = Phase(layer_sems, dict(
            common, am_in=16, wam=1, u_ps=1, hb=2, w1_ps=3, g=FC, w2_ps=1, r2=1, var2=1, rstd2=1, h2=1,
            h_st=16, fl=TOK_FRONT_LINKS, bl=TOK_BACK_LINKS), "t", ("h2", "r2", "h_st"))
        flat_tok = lambda x: x[:].rearrange("p t d -> p (t d)")
        flat_pT = lambda s: pT[s][:].rearrange("p a b -> p (a b)")

        def pe_transposes(src, dst):
            for c in range(2):
                for t in range(T):
                    last = nc.tensor.transpose(dst[0:DC, c * S + t * P:c * S + (t + 1) * P],
                                               src[:, t, c * DC:(c + 1) * DC], eye[:])
            return last

        def pe_qk(ph, pe, F, t):
            s = F.s
            if t == 0:
                ph.wait(pe, "hT", s, F.it)
                if F.wf is not None:
                    pe.wait_ge(w_front, F.wf)
            for c in range(2):
                last = nc.tensor.matmul(bank[s][1 + t][:, 0:2 * D], hT[s][:, c, t * P:(t + 1) * P],
                                        wqkv[:, c, 0:2 * D], start=(c == 0), stop=(c == 1))
            ph.inc(last, "qk_ps", s)

        def pe_v(ph, pe, F):
            s = F.s
            for t in range(T):
                for c in range(2):
                    last = nc.tensor.matmul(bank[s][3][:, t * D:(t + 1) * D], hT[s][:, c, t * P:(t + 1) * P],
                                            wqkv[:, c, 2 * D:3 * D], start=(c == 0), stop=(c == 1))
            ph.inc(last, "v_ps", s)

        def pe_fill(ph, pe, F, f, bank3_key):
            s = F.s
            if f == 0:
                ph.wait(pe, "stk", s, F.it)
            if f == 3:
                ph.wait(pe, bank3_key, s, F.it, 0)
            if f == 4:
                ph.wait(pe, "ev_v", s, F.it, 1)
            if f == 5:
                ph.wait(pe, "ev_s", s, F.it, 1)
            dst = bank[s][f % 4][:].bitcast(BF16)
            side, h0 = f // 3, (f % 3) * 4
            for j in range(4):
                for t in range(T):
                    last = nc.tensor.transpose(dst[:, j * S + t * P:j * S + (t + 1) * P],
                                               stack[s][:, t, side, h0 + j, :], eyeb[:])
            ph.inc(last, "fill", s)

        def pe_scores1(ph, pe, F, h, masks, qcols):
            s = F.s
            if h == 0:
                ph.wait(pe, "ev_v", s, F.it)
                ph.wait(pe, "ev_s", s, F.it)
            if h >= 3:
                ph.wait(pe, "mx", s, F.it, h - 2)
            dst = bank[s][h % 3]
            nc.tensor.matmul(dst[:, 0:SCOLS], eyeb[:], maskb[:, masks, :], start=True, stop=False)
            for t, (c0, f0, w) in enumerate(qcols):
                last = nc.tensor.matmul(dst[:, c0:c0 + w], qT[s][:, h, t * P:(t + 1) * P],
                                        kT[s][:, h, f0:f0 + w], start=False, stop=(t == T - 1))
            ph.inc(last, "sc1", s)

        def pe_maxima(ph, pe, F):
            s = F.s
            ph.wait(pe, "m", s, F.it)
            for f in range(3):
                dst = bank[s][f][:].bitcast(BF16)
                for j in range(4):
                    for t in range(T):
                        last = nc.tensor.transpose(dst[DC:P, j * S + t * P:j * S + (t + 1) * P],
                                                   mrow[s][:, t, f * 4 + j, :], eyeb[:], tile_position=(0, DC))
                ph.inc(last, "mT_ps", s)

        def pe_scores2(ph, pe, K, h, masks, kcols):
            s = K.s
            if h == 0:
                ph.wait(pe, "mT", s, K.it)
            if h >= 2:
                ph.wait(pe, "p", s, K.it, h - 1)
            dst = bank[s][h % 2]
            nc.tensor.matmul(dst[:, 0:SCOLS], eyeb[:], maskb[:, masks + 1, :], start=True, stop=False)
            for t, (c0, f0, w) in enumerate(kcols):
                last = nc.tensor.matmul(dst[:, c0:c0 + w], kT[s][:, h, t * P:(t + 1) * P],
                                        qT[s][:, h, f0:f0 + w], start=False, stop=(t == T - 1))
            ph.inc(last, "sc2", s)

        def pe_product(ph, pe, K, h, kcols):
            s = K.s
            if h == 0:
                ph.wait(pe, "v", s, K.it)
            ph.wait(pe, "p", s, K.it, h + 1)
            g, j = h // 4, h % 4
            dst = bank[s][2 + g // 2]
            at = (g % 2) * S
            (_, _, w0), (c1, f1, w1_) = kcols
            parts = [(0, 0, 0, w0), (1, c1, f1, w0 - f1), (1, c1 + w0 - f1, w0, f1 + w1_ - w0)]
            parts = [part for part in parts if part[3]]
            for n, (t, c0, f0, w) in enumerate(parts):
                last = nc.tensor.matmul(dst[32 * j:32 * j + 32, at + f0:at + f0 + w],
                                        vaug[s][:, t, h, :], pT[s][:, h % NPT, c0:c0 + w],
                                        start=(n == 0), stop=(n == len(parts) - 1), tile_position=(0, 32 * j))
            ph.inc(last, "pv", s)

        def pe_unkept(ph, pe, K):
            s = K.s
            ph.wait(pe, "wam", s, K.it)
            for t in range(T):
                for k in range(T):
                    last = nc.tensor.matmul(
                        bank[s][0][:, t * D:(t + 1) * D], wam[s][:, k, t * P:(t + 1) * P],
                        vaug[s][:, k, :, 0:DH], start=(k == 0), stop=(k == T - 1))
            ph.inc(last, "u_ps", s)

        def pe_output(ph, pe, K):
            s = K.s
            oT = qk[s][:].rearrange("p t s h d -> p (t s h d)")
            ph.wait(pe, "ot", s, K.it)
            for t in range(T):
                for g in range(3):
                    last = nc.tensor.transpose(bank[s][1 + t][:, g * P:(g + 1) * P],
                                               oT[:, g * S + t * P:g * S + (t + 1) * P], eye[:])
                ph.inc(last, "otT_ps", s)

        def pe_att_T(ph, pe, K):
            ph.wait(pe, "att", K.s, K.it)
            ph.inc(pe_transposes(att[K.s], bank[K.s][3]), "aT_ps", K.s)

        def pe_project(ph, pe, K):
            s = K.s
            ph.wait(pe, "aT", s, K.it)
            if K.wb is not None:
                pe.wait_ge(w_back, K.wb)
            for t in range(T):
                for c in range(2):
                    last = nc.tensor.matmul(bank[s][1][:, t * D:(t + 1) * D], hT[s][:, c, t * P:(t + 1) * P],
                                            wo[:, c, :], start=(c == 0), stop=(c == 1))
            ph.inc(last, "wo_ps", s)

        def pe_h1_T(ph, pe, K, src):
            ph.wait(pe, "h1", K.s, K.it)
            ph.inc(pe_transposes(src[K.s], bank[K.s][3]), "h1T_ps", K.s)

        def pe_up(ph, pe, K, f):
            s = K.s
            if f == 0:
                ph.wait(pe, "h1T", s, K.it)
            for c in range(2):
                last = nc.tensor.matmul(bank[s][f // 2][:, (f % 2) * S:(f % 2 + 1) * S],
                                        w1[:, c, f * P:(f + 1) * P], hT[s][:, c, :],
                                        start=(c == 0), stop=(c == 1))
            if f % 2:
                ph.inc(last, "w1_ps", s)

        def pe_down(ph, pe, K):
            s = K.s
            for t in range(T):
                for f in range(FC):
                    if t == 0 and f in (0, FC - 2, FC - 1):
                        ph.wait(pe, "g", s, K.it, max(FC - 2, f + 1))
                    last = nc.tensor.matmul(bank[s][3][:, t * D:(t + 1) * D],
                                            flat_pT(s)[:, f * S + t * P:f * S + (t + 1) * P], w2[:, f, :],
                                            start=(f == 0), stop=(f == FC - 1))
            ph.inc(last, "w2_ps", s)

        def pe_shared_up(ph, pe, K, f):
            s = K.s
            if f == 0:
                ph.wait(pe, "h1T", s, K.it)
                for t in range(T):
                    for c in range(2):
                        last = nc.tensor.matmul(bank[s][3][:, 480 + t * E:480 + (t + 1) * E],
                                                hT[s][:, c, t * P:(t + 1) * P], gw[:, c, :],
                                                start=(c == 0), stop=(c == 1))
                ph.inc(last, "lg_ps", s)
            for side in range(2):
                for c in range(2):
                    last = nc.tensor.matmul(bank[s][f][:, side * S:(side + 1) * S],
                                            w1[:, c, side * FS + f * P:side * FS + (f + 1) * P],
                                            hT[s][:, c, :], start=(c == 0), stop=(c == 1))
            ph.inc(last, "sh_ps", s)

        def pe_shared_down(ph, pe, K):
            s = K.s
            ph.wait(pe, "sig", s, K.it)
            ph.wait(pe, "sh", s, K.it, 1)
            for t in range(T):
                last = nc.tensor.transpose(bank[s][0][0:E, t * P:(t + 1) * P], xr[s][:, t, D:XROW], eye[:])
            ph.inc(last, "sT_ps", s)
            ph.wait(pe, "sh", s, K.it)
            for t in range(T):
                for f in range(FSC):
                    last = nc.tensor.matmul(bank[s][3][:, t * D:(t + 1) * D],
                                            flat_pT(s)[:, (FSC + f) * S + t * P:(FSC + f) * S + (t + 1) * P],
                                            w2[:, f, :], start=(f == 0), stop=(f == FSC - 1))
            ph.inc(last, "dn_ps", s)

        def tensor_half(ph, pe, F, K):
            causal = ph is not tok
            qcols, kcols, masks = (CAUSAL_Q, CAUSAL_K, 2) if causal else (BAND_COLS, BAND_COLS, 0)
            plan, up = (CAUSAL_PLAN, pe_shared_up) if causal else (TOK_PLAN, pe_up)
            for h in range(NH + LAG):
                if K and h < NH:
                    pe_scores2(ph, pe, K, h, masks, kcols)
                if F and h == plan.input:
                    if causal:
                        ph.wait(pe, "sT", F.s, F.it, 0)
                    ph.wait(pe, "x0" if causal else "h_in", F.s, F.it)
                    ph.inc(pe_transposes((h1 if causal else hcur)[F.s], bank[F.s][0]), "hT_ps", F.s)
                if F and h in (plan.qk, plan.qk + 1):
                    pe_qk(ph, pe, F, h - plan.qk)
                if K and h >= LAG:
                    pe_product(ph, pe, K, h - LAG, kcols)
            for f in range(6):
                if K and f == 2:
                    pe_output(ph, pe, K)
                if K and not causal and f == 5:
                    pe_unkept(ph, pe, K)
                if F:
                    pe_fill(ph, pe, F, f, "y" if causal else "r2")
            for h in range(NH):
                if K and h == 0:
                    pe_att_T(ph, pe, K)
                if K and h == plan.proj:
                    pe_project(ph, pe, K)
                if F and h == plan.v:
                    pe_v(ph, pe, F)
                if K and h == plan.h1:
                    pe_h1_T(ph, pe, K, xr if causal else h1)
                if K and h >= plan.up:
                    up(ph, pe, K, h - plan.up)
                if F:
                    pe_scores1(ph, pe, F, h, masks, qcols)
            if F and plan.v == NH:
                pe_v(ph, pe, F)
            if K:
                for f in range(NH - plan.up, FSC if causal else FC):
                    up(ph, pe, K, f)
            if F:
                pe_maxima(ph, pe, F)
            if K:
                (pe_shared_down if causal else pe_down)(ph, pe, K)

        def scalar_half(ph, act, F, K):
            causal = ph is not tok
            plan = CAUSAL_PLAN if causal else TOK_PLAN
            for h in range(NH):
                if K:
                    s = K.s
                    ph.wait(act, "sc2", s, K.it, h + 1)
                    if h >= NPT:
                        ph.wait(act, "pv", s, K.it, h - NPT + 1)
                    ph.inc(nc.scalar.activation(pT[s][:, h % NPT, :], bank[s][h % 2][:, 0:SCOLS], ACT.Exp,
                                                scale=SCALE), "p", s)
                if F and h == plan.input:
                    ph.wait(act, "hT_ps", F.s, F.it)
                    ph.inc(nc.scalar.copy(hT[F.s][:], bank[F.s][0][0:DC, :]), "hT", F.s)
            if K:
                oT = qk[K.s][:].rearrange("p t s h d -> p (t s h d)")
                ph.wait(act, "pv", K.s, K.it)
                nc.scalar.copy(oT[:, 0:2 * S], bank[K.s][2][:])
                ph.inc(nc.scalar.copy(oT[:, 2 * S:3 * S], bank[K.s][3][:, 0:S]), "ot", K.s)
            if F:
                for f in (1, 3, 5):
                    dst = (qT if f < 3 else kT)[F.s][:, (f % 3) * 4:(f % 3) * 4 + 4, :]
                    ph.wait(act, "fill", F.s, F.it, f + 1)
                    ph.inc(nc.scalar.copy(dst, bank[F.s][f % 4][:].bitcast(BF16)), "ev_s", F.s)
            if K:
                s = K.s
                ph.wait(act, "aT_ps", s, K.it)
                ph.inc(nc.scalar.copy(hT[s][:], bank[s][3][0:DC, :]), "aT", s)
                ph.wait(act, "h1T_ps", s, K.it)
                ph.inc(nc.scalar.copy(hT[s][:], bank[s][3][0:DC, :]), "h1T", s)
                if causal:
                    ph.wait(act, "lg_ps", s, K.it)
                    ph.inc(nc.scalar.activation(sig[s][:], bank[s][3][:, 480:512].rearrange("p (t e) -> p t e", e=E),
                                                ACT.Exp, scale=-1.0), "ex", s)
                    for f in range(FSC):
                        ph.wait(act, "sh_ps", s, K.it, f + 1)
                        ph.inc(nc.scalar.activation(flat_pT(s)[:, f * S:(f + 1) * S], bank[s][f][:, 0:S], ACT.Silu),
                               "sg", s)
                else:
                    act.wait_ge(w_back, K.wb)
                    for f in range(FC):
                        ph.wait(act, "w1_ps", s, K.it, f // 2 + 1)
                        ph.inc(nc.scalar.activation(flat_pT(s)[:, f * S:(f + 1) * S],
                                                    bank[s][f // 2][:, (f % 2) * S:(f % 2 + 1) * S],
                                                    ACT.Gelu, bias=b1[:, f:f + 1]), "g", s)
            if K and causal:
                ph.wait(act, "sT_ps", K.s, K.it)
                ph.wait(act, "s_st", K.s, K.it, 0)
                ph.inc(nc.scalar.copy(sT[K.s][:], bank[K.s][0][0:E, 0:S]), "sT", K.s)

        class Chain:

            def __init__(self, ph, dve, turn, key):
                self.ph, self.dve, self.key, self.s, self.k = ph, dve, key, turn.s, 0
                self.base = turn.it * ph.n[key]

            def link(self, fn):
                if self.k:
                    self.wait()
                self.inc(fn())

            def inc(self, ins):
                self.k += 1
                ins.then_inc(self.ph.sem[self.key][self.s], 1)

            def wait(self):
                self.dve.wait_ge(self.ph.sem[self.key][self.s], self.base + self.k)

            def wait_apart(self, held, held_value):
                wait_apart(self.dve, self.ph.sem[self.key][self.s], self.base + self.k, held, held_value)

            def end(self):
                assert self.k == self.ph.n[self.key], (self.key, self.k)

        def norm_stats(ch, x):
            nc.vector.bn_stats(stt[ch.s][:, 0, :], x[:, 0, :])
            ch.inc(nc.vector.bn_stats(stt[ch.s][:, 1, :], x[:, 1, :]))

        def norm_mean(ch):
            s = ch.s
            ch.wait_apart(c_ok, 9)
            nc.vector.bn_aggr(mv[s][:, 0, :], stt[s][:, 0, :])
            ch.inc(nc.vector.bn_aggr(mv[s][:, 1, :], stt[s][:, 1, :]))

        def norm_var(ch, key, eps):
            s = ch.s
            ch.wait()
            ch.ph.inc(nc.vector.tensor_scalar(ve[s][:], mv[s][:, :, 1], eps, None, ALU.add), key, s)

        def norm_scale(ch, it, x, dst, key, done=None):
            s = ch.s
            ch.ph.wait(ch.dve, key, s, it)
            for t in range(T):
                last = nc.vector.tensor_scalar(dst[:, t, :], x[:, t, :], mv[s][:, t, 0:1],
                                               rstd[s][:, t:t + 1], ALU.subtract, ALU.mult)
            ch.inc(last) if done is None else ch.ph.inc(last, done, s)

        def norm_center(ch, x, scale):
            s = ch.s
            for t in range(T):
                last = nc.vector.scalar_tensor_tensor(x[:, t, :], x[:, t, :], mv[s][:, t, 0:1], vec[:, scale:scale + D],
                                                      ALU.subtract, ALU.mult)
            ch.inc(last)

        def norm_finish(ch, it, x, key, shift, done):
            s = ch.s
            ch.ph.wait(ch.dve, key, s, it)
            ch.wait()
            for t in range(T):
                last = nc.vector.scalar_tensor_tensor(x[:, t, :], x[:, t, :], rstd[s][:, t:t + 1], vec[:, shift:shift + D],
                                                      ALU.mult, ALU.add)
            ch.ph.inc(last, done, s)

        def dve_qk(ph, dve, F):
            s = F.s
            if F.wf is not None:
                dve.wait_ge(w_front, F.wf)
            for t in range(T):
                ph.wait(dve, "qk_ps", s, F.it, t + 1)
                ph.inc(nc.vector.tensor_tensor(qk[s][:, t].rearrange("p s h d -> p (s h d)"),
                                               bank[s][1 + t][:, 0:2 * D], vecf[:, 0:2 * D], ALU.add), "qk", s)

        def dve_v(ph, dve, F):
            s = F.s
            ph.wait(dve, "v_ps", s, F.it)
            ph.inc(nc.vector.tensor_tensor(
                vaug[s][:, :, :, 0:DH],
                bank[s][3][:, 0:2 * D].rearrange("p (t h d) -> p t h d", t=T, h=NH),
                vecf[:, 2 * D:3 * D].rearrange("p (h d) -> p h d", h=NH).unsqueeze(1).to_broadcast([P, T, NH, DH]),
                ALU.add), "v", s)

        def rotary(eng, step, s, t):
            even_odd = lambda x, o: x[s][:, t].rearrange("p s h (i e) -> p (s h) i e", e=2)[:, :, :, o]
            heads = lambda x: x[s][:, t].rearrange("p s h d -> p (s h) d")
            step(lambda: eng.tensor_tensor(
                even_odd(rem, 0), even_odd(qk, 1), rope[:, t, 1, 0:8].unsqueeze(1).to_broadcast([P, 2 * NH, 8]),
                ALU.mult))
            step(lambda: eng.tensor_tensor(
                even_odd(rem, 1), even_odd(qk, 0), rope[:, t, 2, 0:8].unsqueeze(1).to_broadcast([P, 2 * NH, 8]),
                ALU.mult))
            step(lambda: eng.tensor_tensor(
                heads(qk), heads(qk), rope[:, t, 0, :].unsqueeze(1).to_broadcast([P, 2 * NH, DH]), ALU.mult))
            step(lambda: eng.tensor_tensor(heads(qk), heads(qk), heads(rem), ALU.add))

        def dve_stack(ph, dve, ch, F, kbcol):
            s = F.s
            flat = lambda x: x[:].rearrange("p t s h d -> p (t s h) d")
            sl = lambda i: stack[s][:].rearrange("p t s h (m d) -> p (t s h) m d", d=DH)[:, :, i, :]
            side = lambda w: stack[s][:, :, w].rearrange("p t h (m d) -> p t h m d", d=DH)
            ph.wait(dve, "qk", s, F.it)
            ch.link(lambda: nc.vector.tensor_copy(sl(0), flat(qk[s])))
            ch.link(lambda: nc.vector.tensor_tensor(flat(rem[s]), flat(qk[s]), sl(0), ALU.subtract))
            ch.link(lambda: nc.vector.tensor_copy(sl(1), flat(rem[s])))
            ch.wait()
            nc.vector.tensor_tensor(side(0)[:, :, :, 5], rem[s][:, :, 0], side(0)[:, :, :, 1], ALU.subtract)
            nc.vector.tensor_tensor(side(1)[:, :, :, 4], rem[s][:, :, 1], side(1)[:, :, :, 1], ALU.subtract)
            for w, dst, src in ((0, 2, 0), (0, 4, 0), (0, 3, 1), (1, 3, 0), (1, 5, 0), (1, 2, 1)):
                nc.vector.tensor_copy(side(w)[:, :, :, dst], side(w)[:, :, :, src])
            ph.inc(nc.vector.tensor_copy(stack[s][:, :, 1, :, DC], kbcol.unsqueeze(2).to_broadcast([P, T, NH])),
                   "stk", s)

        def dve_fill(ph, dve, F, f):
            s = F.s
            dst = (qT if f < 3 else kT)[s][:, (f % 3) * 4:(f % 3) * 4 + 4, :]
            ph.wait(dve, "fill", s, F.it, f + 1)
            ph.inc(nc.vector.tensor_copy(dst, bank[s][f % 4][:].bitcast(BF16)), "ev_v", s)

        def dve_row_max(ph, dve, F, h, qcols):
            s = F.s
            ph.wait(dve, "sc1", s, F.it, h + 1)
            src = bank[s][h % 3]
            if qcols is BAND_COLS:
                last = nc.vector.tensor_reduce(mx[s][:, :, h], src[:, 0:SCOLS].rearrange("p (t k) -> p t k", t=T),
                                               AX, ALU.max)
            else:
                for t, (c0, _, w) in enumerate(qcols):
                    last = nc.vector.tensor_reduce(mx[s][:, t, h:h + 1], src[:, c0:c0 + w], AX, ALU.max)
            ph.inc(last, "mx", s)

        def dve_maxima(ph, dve, ch, F):
            s = F.s
            ph.wait(dve, "mx", s, F.it)
            ch.inc(nc.vector.tensor_scalar(mx[s][:], mx[s][:], M_FLOOR, None, ALU.max))
            ch.link(lambda: nc.vector.tensor_copy(mrow[s][:, :, :, 1], mx[s][:]))
            ch.wait()
            ph.inc(nc.vector.tensor_tensor(mrow[s][:, :, :, 2], mx[s][:], mrow[s][:, :, :, 1], ALU.subtract), "m", s)
            ch.end()

        def dve_maxima_rows(ph, dve, F):
            for f in range(3):
                ph.wait(dve, "mT_ps", F.s, F.it, f + 1)
                ph.inc(nc.vector.tensor_copy(qT[F.s][DC:P, f * 4:f * 4 + 4, :], bank[F.s][f][DC:P, :].bitcast(BF16)),
                       "mT", F.s)

        def o_tokens(s, t):
            return bank[s][1 + t][:, 0:SCOLS].rearrange("p (h d) -> p h d", d=32)

        def dve_sums(ph, dve, ch, K, am):
            s = K.s
            ph.wait(dve, "otT_ps", s, K.it)
            for t in range(T):
                if am is not None:
                    last = nc.vector.tensor_scalar(den[s][:, t], o_tokens(s, t)[:, :, DH], am[:, t:t + 1], None, ALU.add)
                else:
                    last = nc.vector.tensor_copy(den[s][:, t], o_tokens(s, t)[:, :, DH])
            ch.inc(last)
            ch.link(lambda: nc.vector.reciprocal(den[s][:], den[s][:]))

        def dve_divide(ph, dve, ch, K, banded):
            s = K.s
            if not banded:
                ph.wait(dve, "y_st", s, K.it, 0)
            ch.wait()
            for t in range(T):
                last = nc.vector.tensor_tensor(att[s][:, t].rearrange("p (h d) -> p h d", d=DH), o_tokens(s, t)[:, :, 0:DH],
                                               den[s][:, t].unsqueeze(2).to_broadcast([P, NH, DH]), ALU.mult)
            if banded:
                ch.inc(last)
            else:
                ph.inc(last, "att", s)

        def dve_add_unkept(ph, dve, ch, K):
            s = K.s
            ch.wait()
            ph.wait(dve, "u_ps", s, K.it)
            ph.inc(nc.vector.tensor_tensor(flat_tok(att[s]), flat_tok(att[s]), bank[s][0][:, 0:2 * D], ALU.add), "att", s)

        def input_norm_begin(ph, dve, turn):
            ch = Chain(ph, dve, turn, "nl")
            ph.wait(dve, "h_in", turn.s, turn.it)
            norm_stats(ch, hcur[turn.s])
            norm_mean(ch)
            norm_var(ch, "var0", 1e-5)
            ch.end()

        def input_norm_end(ph, dve, turn):
            norm_scale(Chain(ph, dve, turn, "nl"), turn.it, hcur[turn.s], h1[turn.s], "rstd0", "x0")

        def vector_half(ph, dve, F, K):
            causal = ph is not tok
            qcols = CAUSAL_Q if causal else BAND_COLS
            plan = CAUSAL_PLAN if causal else TOK_PLAN
            if F:
                s = F.s
                fc = Chain(ph, dve, F, "fl")
                dve_qk(ph, dve, F)
                if causal:
                    ph.wait(dve, "qk", s, F.it)
                    rotary(nc.vector, fc.link, s, 1)
                    ph.wait(dve, "rot", s, F.it)
                dve_stack(ph, dve, fc, F, kb[:, NT:NT + T] if causal else kb[:, bass.ds(F.pair * (NST * T) + s * T, T)])
                if not causal:
                    ph.wait(dve, "am_in", s, F.it)
                    ph.inc(nc.vector.tensor_tensor(wam[s][:], window[:], amb[s][:].unsqueeze(1).to_broadcast([P, T, S]),
                                                   ALU.mult), "wam", s)
                dve_fill(ph, dve, F, 0)
            if K:
                bc = Chain(ph, dve, K, "bl")
                dve_sums(ph, dve, bc, K, None if causal else amc[:, bass.ds(K.pair * (NST * T) + K.s * T, T)])
            if F:
                dve_fill(ph, dve, F, 2)
            if K:
                dve_divide(ph, dve, bc, K, not causal)
            if F:
                dve_fill(ph, dve, F, 4)
            if K and not causal:
                dve_add_unkept(ph, dve, bc, K)
            for h in range(NH):
                if F:
                    dve_row_max(ph, dve, F, h, qcols)
                if K:
                    s = K.s
                    normed = xr[s][:, :, 0:D] if causal else h1[s]
                    summed = hout[s] if causal else h1[s]
                    if h == plan.res:
                        ph.wait(dve, "wo_ps", s, K.it)
                        ph.wait(dve, "hb", s, K.it, 1)
                        bc.inc(nc.vector.tensor_tensor(flat_tok(summed), bank[s][1][:, 0:2 * D], flat_tok(resid[s]), ALU.add))
                    if h == plan.stats:
                        if causal:
                            ph.wait(dve, "x_st", s, K.it, 0)
                        bc.wait()
                        norm_stats(bc, summed)
                    if h == plan.mean:
                        norm_mean(bc)
                        norm_var(bc, "var1", 1e-5 if causal else 1e-12)
                    if h == plan.center and not causal:
                        dve.wait_ge(w_back, K.wb)
                        norm_center(bc, h1[s], L1S)
                    if h == plan.norm:
                        if causal:
                            norm_scale(bc, K.it, summed, normed, "rstd1", "h1")
                        else:
                            norm_finish(bc, K.it, h1[s], "rstd1", L1B, "h1")
            if F:
                dve_maxima(ph, dve, fc, F)
                dve_v(ph, dve, F)
            if F and not causal:
                dve_maxima_rows(ph, dve, F)
            if K and causal:
                s = K.s
                next_front = K._replace(it=K.it + 1)
                input_norm_begin(ph, dve, next_front)
                ph.wait(dve, "ex", s, K.it)
                bc.link(lambda: nc.vector.tensor_scalar(sig[s][:], sig[s][:], 1.0, None, ALU.add))
                bc.wait()
                ph.inc(nc.vector.reciprocal(xr[s][:, :, D:XROW], sig[s][:]), "sig", s)
                for f in range(FSC):
                    ph.wait(dve, "sg", s, K.it, f + 1)
                    ph.inc(nc.vector.tensor_tensor(flat_pT(s)[:, (FSC + f) * S:(FSC + f + 1) * S],
                                                   flat_pT(s)[:, f * S:(f + 1) * S], bank[s][f][:, S:2 * S], ALU.mult),
                           "sh", s)
                    if f == 0:
                        input_norm_end(ph, dve, next_front)
            if F and causal:
                dve_maxima_rows(ph, dve, F)
            if K and causal:
                s = K.s
                ph.wait(dve, "dn_ps", s, K.it)
                ph.inc(nc.vector.tensor_tensor(flat_tok(att[s]), bank[s][3][:, 0:2 * D], flat_tok(hout[s]), ALU.add), "y", s)
            if K and not causal:
                s = K.s
                ph.wait(dve, "w2_ps", s, K.it)
                ph.wait(dve, "hb", s, K.it, 2)
                ph.wait(dve, "h_st", s, K.it, 0)
                ph.inc(nc.vector.tensor_tensor(flat_tok(hout[s]), bank[s][3][:, 0:2 * D], flat_tok(resid[s]), ALU.add), "r2", s)
                ph.wait(dve, "r2", s, K.it)
                norm_stats(bc, hout[s])
                norm_mean(bc)
                norm_var(bc, "var2", 1e-12)
                norm_center(bc, hout[s], L2S)
                norm_finish(bc, K.it, hout[s], "rstd2", L2B, "h2")
            if K:
                bc.end()

        def input_rstd(ph, pool, s, it):
            ph.wait(pool, "var0", s, it)
            ph.inc(nc.gpsimd.tensor_tensor(rstd[s][:], ve[s][:], half[:], ALU.pow), "rstd0", s)

        def pool_half(ph, pool, F, K):
            causal = ph is not tok
            if F:
                s = F.s
                if causal:
                    ph.wait(pool, "qk", s, F.it, 1)
                    rc = Chain(ph, pool, F, "rot")
                    rotary(nc.gpsimd, rc.link, s, 0)
                    rc.end()
                else:
                    pool.wait_ge(w_front, F.wf)
                ph.wait(pool, "h_in", s, F.it)
                ph.wait(pool, "y" if causal else "h2", s, F.it, 0)
                ph.inc(nc.gpsimd.tensor_tensor(resid[s][:], hcur[s][:],
                                               vecf[:, BO:BO + D].unsqueeze(1).to_broadcast([P, T, D]), ALU.add), "hb", s)
            if K:
                s = K.s
                ph.wait(pool, "var1", s, K.it)
                ph.inc(nc.gpsimd.tensor_tensor(rstd[s][:], ve[s][:], half[:], ALU.pow), "rstd1", s)
                if not causal:
                    pool.wait_ge(w_back, K.wb)
                    ph.wait(pool, "h1", s, K.it)
                    ph.inc(nc.gpsimd.tensor_tensor(resid[s][:], h1[s][:], wide(B2), ALU.add), "hb", s)
                    ph.wait(pool, "var2", s, K.it)
                    ph.inc(nc.gpsimd.tensor_tensor(rstd[s][:], ve[s][:], half[:], ALU.pow), "rstd2", s)
                else:
                    input_rstd(ph, pool, s, K.it + 1)

        def token_layers(eng, half_of):
            half_of(tok, eng, Turn(0, 0, 0, 32, None), None)
            with eng.Fori(0, L) as l:
                wf, wb = (l + 1) * 32, (l + 1) * 80
                with eng.Fori(0, PAIRS - 1) as i:
                    it = l * PAIRS + i
                    half_of(tok, eng, Turn(1, it, i, wf, wb), Turn(0, it, i, wf, wb))
                    half_of(tok, eng, Turn(0, it + 1, i + 1, wf, wb), Turn(1, it, i, wf, wb))
                it = l * PAIRS + (PAIRS - 1)
                half_of(tok, eng, Turn(1, it, PAIRS - 1, wf, wb), Turn(0, it, PAIRS - 1, wf, wb))
                half_of(tok, eng, Turn(0, it + 1, 0, wf + 32, wb), Turn(1, it, PAIRS - 1, wf, wb))

        def causal_layer(eng, half_of, ph):
            half_of(ph, eng, Turn(0, 0, 0, None, None), None)
            with eng.Fori(0, PAIRS - 1) as i:
                half_of(ph, eng, Turn(1, i, i, None, None), Turn(0, i, i, None, None))
                half_of(ph, eng, Turn(0, i + 1, i + 1, None, None), Turn(1, i, i, None, None))
            last = PAIRS - 1
            half_of(ph, eng, Turn(1, last, last, None, None), Turn(0, last, last, None, None))
            half_of(ph, eng, None, Turn(1, last, last, None, None))

        def setup_dve(dve):
            dve.wait_ge(c_in, 16 * 6)
            nc.vector.tensor_copy(eyeb[:], eye[:]).then_inc(c_ok, 1)
            nc.vector.tensor_copy(maskb[:], maskf[:]).then_inc(c_ok, 1)
            nc.vector.memset(kb[:, NT:], 0.0).then_inc(c_ok, 1)
            nc.vector.tensor_scalar(kb[:, 0:NT], kb_i[:], 0, -NEG_KEY, ALU.is_gt, ALU.mult).then_inc(kb_ok, 1)
            dve.wait_ge(kb_ok, 1)
            nc.vector.tensor_scalar(kb[:, 0:NT], kb[:, 0:NT], NEG_KEY, None, ALU.add).then_inc(c_ok, 1)
            for s in ST:
                nc.vector.memset(vaug[s][:], 0.0)
                nc.vector.memset(mrow[s][:], 0.0)
                nc.vector.memset(stack[s][:, :, :, :, DC:], 0.0).then_inc(kb_ok, 1)
            dve.wait_ge(kb_ok, 3)
            for s in ST:
                nc.vector.memset(vaug[s][:, :, :, DH:DH + 1], 1.0)
                nc.vector.memset(mrow[s][:, :, :, 0:1], 1.0)
                nc.vector.memset(stack[s][:, :, 0, :, DC:DC + 1], 1.0)
                nc.vector.memset(stack[s][:, :, 1, :, DC + 1:DC + 3], -1.0).then_inc(c_ok, 1)
            nc.vector.memset(ve[0][:], 1.0).then_inc(c_ok, 1)
            nc.vector.memset(ve[1][:], 1.0).then_inc(c_ok, 1)
            nc.vector.memset(rstd[0][:], 1.0).then_inc(c_ok, 1)
            dve.wait_ge(c_ok, 9)

        with nc.Block() as block:
            @block.sync
            def _(sp):
                sp.dma_start(eye[:], a["c_eye"]).then_inc(c_in, 16)
                sp.dma_start(maskf[:], a["c_masks"].rearrange("m p c -> p m c")).then_inc(c_in, 16)
                sp.dma_start(window[:], a["c_window"]).then_inc(c_in, 16)
                sp.dma_start(rope[:], a["c_rope"]).then_inc(c_in, 16)
                sp.dma_start(kb_i[:], a["mask"].rearrange("b (t p) -> p (b t)", p=P), allow_slow_non_contiguous=True).then_inc(c_in, 16)
                sp.dma_start(amc[:], am_d[0:B, :].rearrange("b (t p) -> p (b t)", p=P), allow_slow_non_contiguous=True).then_inc(c_in, 16)

                def load_h(it_in, s):
                    rows = hbuf[bass.ds(it_in * (NST * S) + s * S, S), :]
                    tok.inc(sp.dma_start(hcur[s][:], rows.rearrange("(t p) d -> p t d", p=P)), "h_in", s)

                def load_am(pair, s):
                    tok.inc(sp.dma_start(amb[s][:], am_d[bass.ds(pair * NST + s, 1), :].to_broadcast([P, S])), "am_in", s)

                def loads(F):
                    s = F.s
                    tok.wait_apart(sp, "hb", s, F.it, 1, c_in, 96)
                    tok.wait(sp, "hT_ps", s, F.it)
                    tok.wait_apart(sp, "h_st", s, F.it, 0, c_in, 96)
                    load_h(F.it + 1, s)
                    tok.wait_apart(sp, "wam", s, F.it, None, c_in, 96)
                    load_am(F.pair + 1, s)

                def store(K):
                    s = K.s
                    tok.wait_apart(sp, "h2", s, K.it, None, c_in, 96)
                    rows = hbuf[bass.ds((K.it + PAIRS) * (NST * S) + s * S, S), :]
                    tok.inc(sp.dma_start(rows.rearrange("(t p) d -> p t d", p=P), hout[s][:]), "h_st", s)

                def load_front(l):
                    sp.dma_start(wqkv[:], a["wqkv"][bass.ds(l, 1)].rearrange("o p c n -> (o p) c n")).then_inc(w_front, 16)
                    sp.dma_start(vecf[:], a["vec"][bass.ds(l, 1), 0:4 * D].to_broadcast([P, 4 * D])).then_inc(w_front, 16)

                def load_back(l):
                    for dst, key in ((wo, "wo"), (w1, "w1"), (w2, "w2")):
                        sp.dma_start(dst[:], a[key][bass.ds(l, 1)].rearrange("o p c n -> (o p) c n")).then_inc(w_back, 16)
                    sp.dma_start(vec[:], a["vec"][bass.ds(l, 1), 4 * D:9 * D].to_broadcast([P, 5 * D])).then_inc(w_back, 16)
                    sp.dma_start(b1[:], a["b1"][bass.ds(l, 1)].rearrange("o p n -> (o p) n")).then_inc(w_back, 16)

                load_front(0)
                for s in ST:
                    load_h(0, s)
                    load_am(0, s)
                load_back(0)
                loads(Turn(0, 0, 0, None, None))
                with sp.Fori(0, L) as l:
                    with sp.Fori(0, PAIRS - 1) as i:
                        it = l * PAIRS + i
                        loads(Turn(1, it, i, None, None))
                        store(Turn(0, it, i, None, None))
                        loads(Turn(0, it + 1, i + 1, None, None))
                        store(Turn(1, it, i, None, None))
                    it = l * PAIRS + (PAIRS - 1)
                    loads(Turn(1, it, PAIRS - 1, None, None))
                    tok.wait(sp, "qk", 1, it)
                    tok.wait(sp, "v", 1, it)
                    load_front(l + 1)
                    store(Turn(0, it, PAIRS - 1, None, None))
                    loads(Turn(0, it + 1, 0, None, None))
                    store(Turn(1, it, PAIRS - 1, None, None))
                    load_back(l + 1)
                sp.wait_ge(w_front, 32 * (L + 1))
                sp.wait_ge(w_back, 80 * (L + 1))
                for s in ST:
                    sp.wait_ge(tok.sem["h_st"][s], 16 * NIT + 1)
                    sp.wait_ge(tok.sem["h_in"][s], 16 * (NIT + 2 - s))
                    sp.wait_ge(tok.sem["am_in"][s], 16 * (NIT + 2 - s))

            @block.gpsimd
            def _(pool):
                nc.gpsimd.memset(half[:], -0.5).then_inc(half_ok, 1)
                pool.wait_ge(half_ok, 1)
                pool.wait_ge(c_ok, 9)
                token_layers(pool, pool_half)

            @block.scalar
            def _(act):
                token_layers(act, scalar_half)

            @block.vector
            def _(dve):
                setup_dve(dve)
                token_layers(dve, vector_half)

            @block.tensor
            def _(pe):
                pe.wait_ge(c_ok, 9)
                token_layers(pe, tensor_half)

        layer_sems.close()
        car = Phase(sem, dict(
            common, x0=1, var0=1, rstd0=1, hb=1, lg_ps=1, ex=1, sig=1, sh_ps=3, sg=3, sh=3, sT_ps=1, sT=1,
            dn_ps=1, y=1, x_st=16, s_st=16, y_st=16, nl=2, rot=4, fl=CAUSAL_FRONT_LINKS, bl=CAUSAL_BACK_LINKS), "c",
            ("y", "sT", "s_st", "x_st", "y_st"))
        y_out = out.rearrange("b s d -> (b s) d")
        with nc.Block() as block:
            @block.sync
            def _(sp):
                sp.dma_start(gw[:], a["gw"]).then_inc(c_in, 16)

                def load_h(i, s):
                    rows = hbuf[bass.ds(i * (NST * S) + (L * N + s * S), S), :]
                    car.inc(sp.dma_start(hcur[s][:], rows.rearrange("(t p) d -> p t d", p=P)), "h_in", s)

                def sync_half(ph, sp, F, K):
                    if F:
                        s = F.s
                        ph.wait(sp, "x0", s, F.it)
                        ph.wait(sp, "hb", s, F.it)
                        load_h(F.it + 1, s)
                    if K:
                        s = K.s
                        rows = bass.ds(K.it * (NST * S) + s * S, S)
                        ph.wait(sp, "sig", s, K.it)
                        ph.inc(sp.dma_start(xs[rows, :].rearrange("(t p) d -> p t d", p=P), xr[s][:]), "x_st", s)
                        ph.wait_apart(sp, "sT", s, K.it, None, c_in, 16 * 7)
                        ph.inc(sp.dma_start(sd[:, rows], sT[s][:]), "s_st", s)
                        ph.wait(sp, "y", s, K.it)
                        ph.inc(sp.dma_start(y_out[rows, :].rearrange("(t p) d -> p t d", p=P), att[s][:]), "y_st", s)
                for s in ST:
                    load_h(0, s)
                causal_layer(sp, sync_half, car)
                for s in ST:
                    for key, n in (("h_in", PAIRS + 1), ("x_st", PAIRS), ("s_st", PAIRS), ("y_st", PAIRS)):
                        sp.wait_ge(car.sem[key][s], 16 * n + (key in car.lifted))

            @block.gpsimd
            def _(pool):
                for s in ST:
                    input_rstd(car, pool, s, 0)
                causal_layer(pool, pool_half, car)

            @block.scalar
            def _(act):
                act.wait_ge(c_in, 16 * 7)
                causal_layer(act, scalar_half, car)

            @block.vector
            def _(dve):
                dve.wait_ge(c_in, 16 * 7)
                for s in ST:
                    input_norm_begin(car, dve, Turn(s, 0, 0, None, None))
                    input_norm_end(car, dve, Turn(s, 0, 0, None, None))
                causal_layer(dve, vector_half, car)

            @block.tensor
            def _(pe):
                pe.wait_ge(c_in, 16 * 7)
                causal_layer(pe, tensor_half, car)


def choose(nc, a, sd, ids_d, N, CAP):
    SEG = P // E
    LEN = N // SEG
    NBLK = LEN // P
    NTILE = SEG * NBLK
    HI = CAP // 32
    with ExitStack() as ctx:
        sb = lambda name, shape, dt: ctx.enter_context(nc.sbuf_tensor("sel_" + name, shape, dt))
        sem = Semaphores(nc)
        sc = sb("sc", [P, LEN], F32)
        same = sb("same", [P, P], F32)
        before = sb("before", [P, P], F32)
        bits = sb("bits", [P, 30], I32)
        iota = sb("iota", [P, 32], F32)
        iotab = sb("iotab", [P, 32], BF16)
        partc = sb("partc", [P, 1], F32)
        tilec = sb("tilec", [P, NTILE], F32)
        tileb = sb("tileb", [P, NTILE], BF16)
        eye = sb("eye_c", [P, P], F32)
        thr = sb("thr", [P, 1], F32)
        cand = sb("cand", [P, 1], F32)
        cnt = sb("cnt", [P, 1], F32)
        flag = sb("flag", [P, 1], F32)
        junk = sb("junk", [P, LEN], F32)
        gt = sb("gt", [P, LEN], F32)
        eq = sb("eq", [P, LEN], F32)
        scan = sb("scan", [P, LEN], F32)
        ones = sb("ones", [P, LEN], F32)
        cnts = sb("cnts", [P, 4], F32)
        slot = sb("slot", [P, LEN], I32)
        part_i = sb("part_i", [P, LEN], I32)
        hilo = sb("hilo", [P, 2, LEN], F32)
        hlT = sb("hlT", [P, 2, NBLK, P], BF16)
        oh_hi = [sb(f"oh_hi{u}", [P, NTILE, 32], BF16) for u in range(2)]
        oh_lo = [sb(f"oh_lo{u}", [P, NTILE, 2, 32], BF16) for u in range(2)]
        ids_f = [sb(f"ids_f{u}", [32, 32], F32) for u in range(2)]
        ids_i = [sb(f"ids_i{u}", [32, 32], I32) for u in range(2)]
        ps_cnt = ctx.enter_context(nc.psum_tensor("ps_cnt", [P, 512], F32))
        ps_tr = [ctx.enter_context(nc.psum_tensor(f"ps_tr{u}", [P, 512], F32)) for u in range(2)]
        ps_id = [ctx.enter_context(nc.psum_tensor(f"ps_id{u}", [P, 512], F32)) for u in range(2)]
        tab_in, thr0, cand_ok, cnt_ok, tot_ok, flag_ok, thr_ok = (
            sem("s_tab"), sem("s_thr0"), sem("s_cand"), sem("s_cnt"), sem("s_tot"), sem("s_flag"), sem("s_thr"))
        if_ok = [sem(f"s_if{u}") for u in range(2)]
        chain, blk_in, blk_out, hl_ok, tr_ok, hlT_ok = (sem("s_chain"), sem("s_bin"), sem("s_bout"),
                                                        sem("s_hl"), sem("s_tr"), sem("s_hlT"))
        oh_ok, idp_ok, idi_ok, ids_st = ([sem(f"s_oh{u}") for u in range(2)], [sem(f"s_idp{u}") for u in range(2)],
                                         [sem(f"s_idi{u}") for u in range(2)], [sem(f"s_ids{u}") for u in range(2)])
        oc, hi_ok, by_tile = [sem(f"s_oc{u}") for u in range(2)], [sem(f"s_hi{u}") for u in range(2)], sem("s_tile")
        ctx.callback(sem.close)
        sem.lift([thr_ok] + idp_ok + idi_ok + ids_st)
        block = ctx.enter_context(nc.Block())

        @block.sync
        def _(sp):
            sp.dma_start(sc[:], sd.rearrange("e (s n) -> (e s) n", n=LEN)).then_inc(tab_in, 16)
            for dst, key in ((same, "c_same"), (before, "c_before"), (bits, "c_bits"), (iota, "c_iota"),
                             (partc, "c_part"), (tilec, "c_tile"), (eye, "c_eye")):
                sp.dma_start(dst[:], a[key]).then_inc(tab_in, 16)
            with sp.Fori(0, E // 2) as i:
                for u in range(2):
                    sp.wait_ge(idi_ok[u], i + 2)
                    dst = ids_d[bass.ds(i * 2 + u, 1), :].rearrange("o (h l) -> (o h) l", l=32)
                    sp.dma_start(dst, ids_i[u][:]).then_inc(ids_st[u], 16)
            for u in range(2):
                sp.wait_ge(ids_st[u], 16 * (E // 2) + 1)

        @block.vector
        def _(dve):
            dve.wait_ge(tab_in, 16 * 8)
            nc.vector.memset(thr[:], 0.0)
            nc.vector.memset(ones[:], 1.0)
            nc.vector.tensor_copy(iotab[:], iota[:])
            nc.vector.tensor_copy(tileb[:], tilec[:]).then_inc(thr0, 1)
            dve.wait_ge(thr0, 1)
            with dve.Fori(0, 30) as k:
                dve.wait_ge(thr_ok, k + 1)
                nc.vector.tensor_tensor(cand[:].bitcast(I32), thr[:].bitcast(I32), bits[:, bass.ds(k, 1)],
                                        ALU.bitwise_or).then_inc(cand_ok, 1)
                dve.wait_ge(cand_ok, k + 1)
                nc.vector.tensor_scalar(junk[:], sc[:], cand[:], 0.0, ALU.is_ge, ALU.add,
                                        accum_out=cnt[:]).then_inc(cnt_ok, 1)
                dve.wait_ge(tot_ok, k + 1)
                nc.vector.tensor_scalar(flag[:], ps_cnt[:, 0:1], float(CAP), None, ALU.is_ge).then_inc(flag_ok, 1)
                dve.wait_ge(flag_ok, k + 1)
                nc.vector.scalar_tensor_tensor(out=thr[:], in0=cand[:], scalar=flag[:], in1=thr[:],
                                               op0=ALU.mult, op1=ALU.max).then_inc(thr_ok, 1)
            dve.wait_ge(thr_ok, 31)
            n = [0]

            def link(ins):
                n[0] += 1
                ins.then_inc(chain, 1)
                dve.wait_ge(chain, n[0])
            link(nc.vector.tensor_scalar(gt[:], sc[:], thr[:], 0.0, ALU.is_gt, ALU.add, accum_out=cnts[:, 0:1]))
            link(nc.vector.tensor_scalar(eq[:], sc[:], thr[:], 0.0, ALU.is_equal, ALU.add, accum_out=cnts[:, 1:2]))
            nc.vector.tensor_tensor_scan(scan[:], ones[:], eq[:], 0.0, ALU.mult, ALU.add).then_inc(blk_in, 1)
            dve.wait_ge(blk_out, 1)
            dve.wait_ge(blk_in, 1)
            link(nc.vector.tensor_copy(cnts[:, 0:2], ps_cnt[:, 0:2]))
            link(nc.vector.tensor_tensor(cnts[:, 2:3], cnts[:, 0:1], cnts[:, 1:2], ALU.add))
            link(nc.vector.tensor_scalar(cnts[:, 2:3], cnts[:, 2:3], -1.0, float(CAP), ALU.mult, ALU.add))
            link(nc.vector.tensor_scalar(scan[:], scan[:], cnts[:, 2:3], None, ALU.is_le))
            link(nc.vector.tensor_tensor(eq[:], eq[:], scan[:], ALU.mult))
            link(nc.vector.tensor_tensor(gt[:], gt[:], eq[:], ALU.add))
            link(nc.vector.tensor_tensor_scan(scan[:], ones[:], gt[:], 0.0, ALU.mult, ALU.add))
            nc.vector.tensor_copy(cnts[:, 3:4], scan[:, LEN - 1:LEN]).then_inc(blk_in, 1)
            dve.wait_ge(blk_out, 2)
            link(nc.vector.tensor_scalar(scan[:], scan[:], ps_cnt[:, 2:3], -2048.0, ALU.add, ALU.add))
            link(nc.vector.tensor_tensor(scan[:], scan[:], gt[:], ALU.mult))
            link(nc.vector.tensor_scalar(slot[:], scan[:], 2047.0, None, ALU.add))
            link(nc.vector.tensor_scalar(part_i[:], slot[:], 5, None, ALU.arith_shift_right))
            link(nc.vector.tensor_copy(hilo[:, 0, :], part_i[:]))
            link(nc.vector.tensor_scalar(part_i[:], slot[:], 31, None, ALU.bitwise_and))
            nc.vector.tensor_copy(hilo[:, 1, :], part_i[:]).then_inc(hl_ok, 1)
            for w in range(2):
                for c in range(NBLK // 4 if NBLK >= 4 else 1):
                    k = w * max(NBLK // 4, 1) + c
                    nb = min(4, NBLK)
                    dve.wait_ge(tr_ok, k + 1)
                    nc.vector.tensor_copy(hlT[:, w, c * 4:c * 4 + nb, :].rearrange("p c r -> p (c r)"),
                                          ps_tr[k % 2][:, 0:nb * P]).then_inc(hlT_ok, 1)
            dve.wait_ge(hlT_ok, 2 * max(NBLK // 4, 1))

            def tables(i):
                for u in range(2):
                    dve.wait_ge(idp_ok[u], i + 1)
                    rows = bass.ds((i * 2 + u) * SEG, SEG)
                    grid = [P, NBLK, SEG, 32]
                    lane = iotab[:].unsqueeze(1).unsqueeze(1).to_broadcast(grid)
                    hi = oh_hi[u][:].rearrange("p (c s) l -> p c s l", s=SEG)
                    lo = oh_lo[u][:].rearrange("p (c s) w l -> p c s w l", s=SEG)
                    nc.vector.tensor_tensor(lo[:, :, :, 0, :], lane, hlT[:, 1, :, rows].unsqueeze(3).to_broadcast(grid),
                                            ALU.is_equal).then_inc(oc[u], 1)
                    nc.vector.tensor_tensor(hi, lane, hlT[:, 0, :, rows].unsqueeze(3).to_broadcast(grid),
                                            ALU.is_equal).then_inc(hi_ok[u], 1)
                dve.wait_ge(oc[1], i * 2 + 1)
                nc.vector.tensor_tensor(oh_lo[1][:, :, 1, :], oh_lo[1][:, :, 0, :],
                                        tileb[:].unsqueeze(2).to_broadcast([P, NTILE, 32]), ALU.mult).then_inc(oc[1], 1)
                for u in range(2):
                    if u == 0:
                        dve.wait_ge(by_tile, i + 1)
                    else:
                        dve.wait_ge(oc[1], i * 2 + 2)
                    nc.vector.tensor_scalar(oh_lo[u][:, :, 0, :], oh_lo[u][:, :, 0, :], partc[:], None,
                                            ALU.mult).then_inc(oh_ok[u], 1)

            def read_ids(i):
                for u in range(2):
                    dve.wait_ge(idp_ok[u], i + 2)
                    nc.vector.tensor_copy(ids_f[u][:], ps_id[u][0:32, 0:32]).then_inc(if_ok[u], 1)
                for u in range(2):
                    dve.wait_ge(if_ok[u], i + 1)
                    dve.wait_ge(ids_st[u], i * 16 + 1)
                    nc.vector.scalar_tensor_tensor(out=ids_i[u][:], in0=ps_id[u][0:32, 32:64], scalar=float(P),
                                                   in1=ids_f[u][:], op0=ALU.mult, op1=ALU.add).then_inc(idi_ok[u], 1)
            tables(0)
            with dve.Fori(1, E // 2) as i:
                tables(i)
                read_ids(i - 1)
            read_ids(E // 2 - 1)

        @block.gpsimd
        def _(pool):
            with pool.Fori(0, E // 2) as i:
                pool.wait_ge(oc[0], i + 1)
                nc.gpsimd.tensor_tensor(oh_lo[0][:, :, 1, :], oh_lo[0][:, :, 0, :],
                                        tileb[:].unsqueeze(2).to_broadcast([P, NTILE, 32]), ALU.mult).then_inc(by_tile, 1)

        @block.tensor
        def _(pe):
            pe.wait_ge(tab_in, 16 * 8)
            with pe.Fori(0, 30) as k:
                pe.wait_ge(cnt_ok, k + 1)
                nc.tensor.matmul(ps_cnt[:, 0:1], same[:], cnt[:], start=True, stop=True).then_inc(tot_ok, 1)
            pe.wait_ge(blk_in, 1)
            pe.wait_ge(chain, 2)
            pe.wait_ge(thr_ok, 31)
            nc.tensor.matmul(ps_cnt[:, 0:1], same[:], cnts[:, 0:1], start=True, stop=True)
            nc.tensor.matmul(ps_cnt[:, 1:2], before[:], cnts[:, 1:2], start=True, stop=True).then_inc(blk_out, 1)
            pe.wait_ge(blk_in, 2)
            nc.tensor.matmul(ps_cnt[:, 2:3], before[:], cnts[:, 3:4], start=True, stop=True).then_inc(blk_out, 1)
            pe.wait_ge(hl_ok, 1)
            nf = max(NBLK // 4, 1)
            for w in range(2):
                for c in range(nf):
                    k = w * nf + c
                    if k >= 2:
                        pe.wait_ge(hlT_ok, k - 1)
                    for j in range(min(4, NBLK)):
                        blk = c * 4 + j
                        last = nc.tensor.transpose(ps_tr[k % 2][:, j * P:(j + 1) * P],
                                                   hilo[:, w, blk * P:(blk + 1) * P], eye[:])
                    last.then_inc(tr_ok, 1)
            with pe.Fori(0, E // 2) as i:
                for u in range(2):
                    pe.wait_ge(oh_ok[u], i + 1)
                    pe.wait_ge(hi_ok[u], i + 1)
                    pe.wait_ge(idi_ok[u], i + 1)
                    for t in range(NTILE):
                        last = nc.tensor.matmul(ps_id[u][0:32, 0:64], oh_hi[u][:, t, :],
                                                oh_lo[u][:, t].rearrange("p w l -> p (w l)"),
                                                start=(t == 0), stop=(t == NTILE - 1))
                    last.then_inc(idp_ok[u], 1)


def experts(nc, a, xs, ids_d, out, N, CAP):
    G = CAP // P
    HALF = 512
    NHALF = CAP // HALF
    y_out = out.rearrange("b s d -> (b s) d")
    U = (0, 1)
    with ExitStack() as ctx:
        sb = lambda name, shape, dt: ctx.enter_context(nc.sbuf_tensor("exp_" + name, shape, dt))
        sem = Semaphores(nc)
        eye = sb("eye_x", [P, P], F32)
        wg = [sb(f"wg{u}", [DC, 2, FF], F32) for u in U]
        wu = [sb(f"wu{u}", [DC, 2, FF], F32) for u in U]
        wd = [sb(f"wd{u}", [P, FC, D], F32) for u in U]
        idx = [sb(f"idx{u}", [P, G], I32) for u in U]
        xg = [sb(f"xg{u}", [P, G, XROW], F32) for u in U]
        xT = sb("xT", [DC, 2, CAP], F32)
        hid = sb("hid", [P, NHALF, FC, HALF], F32)
        sg = [sb(f"sg{u}", [P, HALF], F32) for u in U]
        yb = [sb(f"yb{u}", [P, G, D], F32) for u in U]
        ps_x = [ctx.enter_context(nc.psum_tensor(f"ps_x{i}", [P, 512], F32)) for i in range(2)]
        ps_g = [ctx.enter_context(nc.psum_tensor(f"ps_g{i}", [P, 512], F32)) for i in range(2)]
        ps_u = [ctx.enter_context(nc.psum_tensor(f"ps_u{i}", [P, 512], F32)) for i in range(2)]
        ps_y = [ctx.enter_context(nc.psum_tensor(f"ps_y{i}", [P, 512], F32)) for i in range(2)]
        eye_in = sem("x_eye")
        w_in = [sem(f"x_w{u}") for u in U]
        i_in = [sem(f"x_i{u}") for u in U]
        g_in = [sem(f"x_g{u}") for u in U]
        xT_ps, xT_v, xT_s, gu_ps, sg_ok, hid_ok, y_ps, y_ok = (sem("x_xTp"), sem("x_xTv"), sem("x_xTs"), sem("x_gup"),
                                                                sem("x_sg"), sem("x_hid"), sem("x_yp"), sem("x_y"))
        y_st = sem("x_yst")
        NX = G // 2
        NF = NHALF * FC
        ctx.callback(sem.close)
        sem.lift([y_ok, hid_ok])
        block = ctx.enter_context(nc.Block())

        @block.sync
        def _(sp):
            sp.dma_start(eye[:], a["c_eye"]).then_inc(eye_in, 16)

            def load(e, u):
                one = bass.ds(e, 1)
                sp.dma_start(idx[u][:], ids_d[one, :].rearrange("o (p g) -> (o p) g", g=G)).then_inc(i_in[u], 16)
                for dst, key in ((wg, "ewg"), (wu, "ewu"), (wd, "ewd")):
                    sp.dma_start(dst[u][:], a[key][one].rearrange("o p c n -> (o p) c n")).then_inc(w_in[u], 16)
            for u in U:
                load(u, u)
            with sp.Fori(0, E // 2 - 1) as i:
                for u in U:
                    sp.wait_ge(y_st, (i * 2 + u + 1) * (16 * G))
                    load(i * 2 + u + 2, u)
            sp.wait_ge(y_st, 16 * G * E)

        @block.gpsimd
        def _(pool):
            def gather(i, u):
                wait_apart(pool, i_in[u], i * 16 + 16, eye_in, 16)
                for g in range(G):
                    pool.indirect_dma_start(xg[u][:, g, :], None, xs,
                                            bass.IndirectOffsetOnAxis(ap=idx[u][:, g:g + 1], axis=0)
                                            ).then_inc(g_in[u], 16)

            def scatter(i, u):
                if not (isinstance(i, int) and i * 2 + u == 0):
                    pool.wait_ge(y_st, (i * 2 + u) * (16 * G))
                for g in range(G):
                    if g % 2 == 0:
                        wait_apart(pool, y_ok, (i * 2 + u) * NX + (g // 2 + 2), eye_in, 16)
                    pool.indirect_dma_start(y_out, bass.IndirectOffsetOnAxis(ap=idx[u][:, g:g + 1], axis=0),
                                            yb[u][:, g, :], None, compute_op=ALU.add).then_inc(y_st, 16)
            pool.wait_ge(eye_in, 16)
            gather(0, 0)
            gather(0, 1)
            for u in U:
                scatter(0, u)
                gather(1, u)
            with pool.Fori(1, E // 2 - 1) as i:
                for u in U:
                    scatter(i, u)
                    gather(i + 1, u)
            for u in U:
                scatter(E // 2 - 1, u)

        @block.scalar
        def _(act):
            def read_xT(e):
                for k in range(1, NX, 2):
                    act.wait_ge(xT_ps, e * NX + k + 1)
                    nc.scalar.copy(xT[:, :, k * 2 * P:(k + 1) * 2 * P], ps_x[k % 2][0:DC, :].rearrange("p (c n) -> p c n", c=2)
                                   ).then_inc(xT_s, 1)

            def gates(e):
                for k in range(NF):
                    act.wait_ge(gu_ps, e * NF + k + 1)
                    act.wait_ge(hid_ok, e * NF + max(k, 1))
                    nc.scalar.activation(sg[k % 2][:], ps_g[k % 2][:], ACT.Silu).then_inc(sg_ok, 1)
            read_xT(0)
            with act.Fori(0, E // 2 - 1) as i:
                for u in U:
                    gates(i * 2 + u)
                    read_xT(i * 2 + (u + 1))
            gates(E - 2)
            read_xT(E - 1)
            gates(E - 1)

        @block.vector
        def _(dve):
            def read_xT(e):
                for k in range(0, NX, 2):
                    dve.wait_ge(xT_ps, e * NX + k + 1)
                    nc.vector.tensor_copy(xT[:, :, k * 2 * P:(k + 1) * 2 * P],
                                          ps_x[k % 2][0:DC, :].rearrange("p (c n) -> p c n", c=2)).then_inc(xT_v, 1)

            def hidden(e):
                for k in range(NF):
                    dve.wait_ge(sg_ok, e * NF + k + 1)
                    nc.vector.tensor_tensor(hid[:, k // FC, k % FC, :], sg[k % 2][:], ps_u[k % 2][:], ALU.mult
                                            ).then_inc(hid_ok, 1)

            def weigh(e, u):
                for k in range(NX):
                    dve.wait_ge(y_ps, e * NX + k + 1)
                    for j in range(2):
                        g = 2 * k + j
                        last = nc.vector.tensor_scalar(yb[u][:, g, :], ps_y[k % 2][:, j * D:(j + 1) * D],
                                                       xg[u][:, g, bass.ds(e + D, 1)], None, ALU.mult)
                    last.then_inc(y_ok, 1)
            read_xT(0)
            with dve.Fori(0, E // 2 - 1) as i:
                for u in U:
                    hidden(i * 2 + u)
                    read_xT(i * 2 + (u + 1))
                    weigh(i * 2 + u, u)
            hidden(E - 2)
            read_xT(E - 1)
            weigh(E - 2, 0)
            hidden(E - 1)
            weigh(E - 1, 1)

        @block.tensor
        def _(pe):
            def transposes(i, u):
                e = i * 2 + u
                pe.wait_ge(g_in[u], i * (16 * G) + 16 * G)
                for k in range(NX):
                    if k >= 2:
                        pe.wait_ge(xT_s if k % 2 else xT_v, e * (NX // 2) + k // 2)
                    for c in range(2):
                        for j in range(2):
                            last = nc.tensor.transpose(ps_x[k % 2][0:DC, c * 2 * P + j * P:c * 2 * P + (j + 1) * P],
                                                       xg[u][:, 2 * k + j, c * DC:(c + 1) * DC], eye[:])
                    last.then_inc(xT_ps, 1)

            def gate_up(i, u):
                e = i * 2 + u
                pe.wait_ge(xT_v, (e + 1) * (NX // 2))
                pe.wait_ge(xT_s, (e + 1) * (NX // 2))
                pe.wait_ge(w_in[u], i * 48 + 48)
                for k in range(NF):
                    n0, f = (k // FC) * HALF, k % FC
                    pe.wait_ge(hid_ok, e * NF + max(k, 1))
                    for w, dst in ((wg, ps_g), (wu, ps_u)):
                        for c in range(2):
                            last = nc.tensor.matmul(dst[k % 2][:], w[u][:, c, f * P:(f + 1) * P],
                                                    xT[:, c, n0:n0 + HALF], start=(c == 0), stop=(c == 1))
                    last.then_inc(gu_ps, 1)

            def down(i, u):
                e = i * 2 + u
                pe.wait_ge(hid_ok, e * NF + (NF + 1))
                for k in range(NX):
                    pe.wait_ge(y_ok, e * NX + max(k, 1))
                    for j in range(2):
                        g = 2 * k + j
                        n0, o = g * P // HALF, g * P % HALF
                        for f in range(FC):
                            last = nc.tensor.matmul(ps_y[k % 2][:, j * D:(j + 1) * D], hid[:, n0, f, o:o + P],
                                                    wd[u][:, f, :], start=(f == 0), stop=(f == FC - 1))
                    last.then_inc(y_ps, 1)
            pe.wait_ge(eye_in, 16)
            transposes(0, 0)
            with pe.Fori(0, E // 2 - 1) as i:
                gate_up(i, 0)
                transposes(i, 1)
                down(i, 0)
                gate_up(i, 1)
                transposes(i + 1, 0)
                down(i, 1)
            last_pair = E // 2 - 1
            gate_up(last_pair, 0)
            transposes(last_pair, 1)
            down(last_pair, 0)
            gate_up(last_pair, 1)
            down(last_pair, 1)


def kernel(**inputs):
    import concourse.bacc as bacc
    from concourse.bass_utils import run_bass_kernel_spmd

    g = {k: np.asarray(v) for k, v in inputs.items()}
    tok = {k[len("L0_tok_"):]: v for k, v in g.items() if k.startswith("L0_tok_")}
    B = g["x"].shape[0]
    L = tok["Wq"].shape[0]
    V = tok["emb_word"].shape[0]
    chunks = lambda w, p: np.swapaxes(w.reshape(w.shape[:-2] + (w.shape[-2] // p, p, w.shape[-1])), -3, -2)
    tr = lambda w: np.swapaxes(w, -1, -2)
    z = lambda n: np.zeros(n, np.float32)
    one = lambda w: w[None]
    wqkv = np.concatenate([np.concatenate([tok["Wq"], tok["Wk"], tok["Wv"]], -1), one(g["L0_attn_W_attn"])])
    wo = np.concatenate([tok["Wo"], one(g["L0_attn_W_proj"])])
    w1 = np.concatenate([tok["W1"], one(np.concatenate([tr(g["L0_ffn_Ws_g"]), tr(g["L0_ffn_Ws_u"])], -1))])
    w2 = np.concatenate([tok["W2"], one(np.concatenate([tr(g["L0_ffn_Ws_d"]), z((FF - FS, D))]))])
    vec = np.concatenate([
        np.concatenate([tok[k] for k in ("bq", "bk", "bv", "bo", "ln1_s", "ln1_b", "b2", "ln2_s", "ln2_b")], -1),
        one(np.concatenate([g["L0_attn_b_attn"], g["L0_attn_b_proj"], z(5 * D)]))])
    b1 = np.concatenate([tok["b1"], z((1, FF))]).reshape(L + 1, FC, P)
    arrays = {
        "x": g["x"], "mask": g["mask_BS_i1_0"], "emb_word": tok["emb_word"], "emb_pos": tok["emb_pos"][:S],
        "emb_ln": one(np.concatenate([tok["emb_ln_s"], tok["emb_ln_b"]])),
        "wqkv": chunks(wqkv, DC), "wo": chunks(wo, DC), "w1": chunks(w1, DC), "w2": chunks(w2, P), "vec": vec,
        "b1": tr(b1), "gw": chunks(tr(g["L0_ffn_gate_weight"]), DC), "ewg": chunks(tr(g["L0_ffn_Wg"]), DC),
        "ewu": chunks(tr(g["L0_ffn_Wu"]), DC), "ewd": chunks(tr(g["L0_ffn_Wd"]), P),
    }
    arrays.update(constants())
    arrays.update(select_constants(B * S, P // E))
    nc = bacc.Bacc("TRN2", target_bir_lowering=False, num_devices=1)
    feed, aps = {}, {}
    for name, v in arrays.items():
        v = np.ascontiguousarray(v)
        feed[f"in_{name}"] = v
        aps[name] = nc.dram_tensor(f"in_{name}", list(v.shape), mybir.dt.from_np(v.dtype), kind="ExternalInput").ap()
    out = nc.dram_tensor("out", [B, S, D], F32, kind="ExternalOutput").ap()
    build(nc, aps, out, B, L, V)
    r = run_bass_kernel_spmd(nc, [feed], core_ids=[0])
    return r.results[0]["out"]
```
